# Optimizing a Trainium2 kernel written in Bass

```python
import numpy as np
import jax
import jax.numpy as jnp

def _softmax(x, axis=-1):
    return jax.nn.softmax(x, axis=axis)

def _gelu(x):
    return jax.nn.gelu(x, approximate=True)

def _silu(x):
    return jax.nn.silu(x)

def _sigmoid(x):
    return jax.nn.sigmoid(x)

def _layernorm(x, axis=-1, eps=1e-05):
    m = jnp.mean(x, axis=axis, keepdims=True)
    v = jnp.var(x, axis=axis, keepdims=True)
    return (x - m) / jnp.sqrt(v + eps)

def _scatter_add(tgt, idx, src, axis=0):
    return tgt.at[idx].add(src)

def _segment_sum(src, seg, n):
    return jax.ops.segment_sum(src, seg, n)
kernel_name = 'mk_cond_resid_d2_seqx_r2_440241'

def setup_inputs(seed: int=0):
    np.random.seed(seed)
    _w = jnp.asarray

    def _rec_inputs():
        import jax
        import jax.numpy as jnp
        _rk = jax.random.key(seed)
        x = 7.22e-05 + 1 * jax.random.normal(jax.random.fold_in(_rk, 1), (4, 1024, 512), jnp.float32)
        _lenS = 1024 - jax.random.randint(jax.random.fold_in(_rk, 7), (4,), 0, max(1, 1024 // 4) + 1, jnp.int32)
        _lenS2 = 1024 - jax.random.randint(jax.random.fold_in(_rk, 8), (4,), 0, max(1, 1024 // 4) + 1, jnp.int32)
        cond_512 = 0.0061147 + 1.02565 * jax.random.normal(jax.random.fold_in(_rk, 11), (4, 256), jnp.float32)
        itok_BxS_0_999 = jax.random.randint(jax.random.fold_in(_rk, 12), (4, 1024), 0, 500, jnp.int32)
        itok_BxS_0_4 = jax.random.randint(jax.random.fold_in(_rk, 13), (4, 1024), 0, 5, jnp.int32)
        cond_64 = 0.0990542 + 1.04422 * jax.random.normal(jax.random.fold_in(_rk, 15), (4, 64), jnp.float32)
        fside_Bx32_0 = -0.136436 + 0.990155 * jax.random.normal(jax.random.fold_in(_rk, 16), (4, 32), jnp.float32)
        _validS = jnp.arange(1024)[None, :] < _lenS[:, None]
        _validS2 = jnp.arange(1024)[None, :] < _lenS2[:, None]
        _causal = jnp.tril(jnp.ones((1024, 1024), dtype=bool))
        mask_BxS_ik0 = jnp.where(jnp.broadcast_to(_validS[:, :], (4, 1024)), 0, 1).astype(jnp.int32)
        return (x, cond_512, itok_BxS_0_999, itok_BxS_0_4, cond_64, fside_Bx32_0, mask_BxS_ik0)
    x, cond_512, itok_BxS_0_999, itok_BxS_0_4, cond_64, fside_Bx32_0, mask_BxS_ik0 = _rec_inputs()

    def _L0_cond_setup():
        import jax, jax.numpy as jnp
        import numpy as np
        import math
        HEAD_NUM = 16
        EPS = 1e-08

        def modulated_linear(x, s, aff_w, aff_b, w, b):
            style = s @ aff_w.T + aff_b
            w_mod = w[None, :, :] * style[:, None, :]
            demod = jax.lax.rsqrt(jnp.sum(w_mod * w_mod, axis=2) + EPS)
            w_mod = w_mod * demod[:, :, None]
            return jnp.einsum('bni,boi->bno', x, w_mod) + b
        key = jax.random.key(seed)
        ks = jax.random.split(key, 6)
        B, N, F, S = (8, 512, 512, 256)
        return {'x': jax.random.normal(ks[0], (B, N, F), dtype=jnp.float32), 's': jax.random.normal(ks[1], (B, S), dtype=jnp.float32), 'k_aff_w': jax.random.normal(ks[2], (F, S), dtype=jnp.float32) * 0.02, 'k_aff_b': jnp.ones((F,), dtype=jnp.float32), 'k_w': jax.random.normal(ks[3], (F, F), dtype=jnp.float32) * 0.02, 'k_b': jnp.zeros((F,), dtype=jnp.float32), 'o_aff_w': jax.random.normal(ks[4], (F, S), dtype=jnp.float32) * 0.02, 'o_aff_b': jnp.ones((F,), dtype=jnp.float32), 'o_w': jax.random.normal(ks[5], (F, F), dtype=jnp.float32) * 0.02, 'o_b': jnp.zeros((F,), dtype=jnp.float32)}
    _L0_cond_all = _L0_cond_setup()
    _L0_cond_in = {k: v for k, v in _L0_cond_all.items() if k in ('k_aff_w', 'k_aff_b', 'k_w', 'k_b', 'o_aff_w', 'o_aff_b', 'o_w', 'o_b')}
    del _L0_cond_all

    def _L1_cond_setup():
        import jax, jax.numpy as jnp
        import numpy as np
        EPS = 1e-05

        def _ln(x, g, b):
            m = jnp.mean(x, axis=-1, keepdims=True)
            v = jnp.mean((x - m) ** 2, axis=-1, keepdims=True)
            return (x - m) * jax.lax.rsqrt(v + EPS) * g + b

        def _mlp_ln(s, W1, b1, W2, b2, g, b):
            h = jax.nn.silu(s @ W1 + b1) @ W2 + b2
            return _ln(h, g, b)
        key = jax.random.key(seed)
        B, S, D = (4, 1024, 512)
        MEM, NOI, RES = (256, 64, 32)
        ks = jax.random.split(key, 40)
        ki = iter(range(40))

        def nrm(shape, scale=0.02):
            return jax.random.normal(ks[next(ki)], shape, jnp.float32) * scale

        def gamma(shape):
            return jnp.ones(shape, jnp.float32) + nrm(shape)
        inp = {'x': jax.random.normal(ks[next(ki)], (B, S, D), jnp.float32), 'pathway_ids': jax.random.randint(ks[next(ki)], (B, S), 0, 500), 'compartment_ids': jax.random.randint(ks[next(ki)], (B, S), 0, 5), 'time_steps': jax.random.randint(ks[next(ki)], (B, S), 0, 5), 'scale_type': jax.random.randint(ks[next(ki)], (B, S), 0, 3), 'memory_state': jax.random.normal(ks[next(ki)], (B, MEM), jnp.float32), 'noise_state': jax.random.normal(ks[next(ki)], (B, NOI), jnp.float32), 'resource_state': jax.random.normal(ks[next(ki)], (B, RES), jnp.float32), 'pw_g': gamma((500, D)), 'pw_b': nrm((500, D)), 'cp_g': gamma((5, D)), 'cp_b': nrm((5, D)), 'tm_g': gamma((5, D)), 'tm_b': nrm((5, D)), 'ms_g': gamma((3, D)), 'ms_b': nrm((3, D)), 'mem_W1': nrm((MEM, D)), 'mem_b1': jnp.zeros((D,)), 'mem_W2': nrm((D, D)), 'mem_b2': jnp.zeros((D,)), 'mem_g': gamma((D,)), 'mem_be': jnp.zeros((D,)), 'noi_W1': nrm((NOI, D)), 'noi_b1': jnp.zeros((D,)), 'noi_W2': nrm((D, D)), 'noi_b2': jnp.zeros((D,)), 'noi_g': gamma((D,)), 'noi_be': jnp.zeros((D,)), 'res_W1': nrm((RES, D)), 'res_b1': jnp.zeros((D,)), 'res_W2': nrm((D, D)), 'res_b2': jnp.zeros((D,)), 'res_g': gamma((D,)), 'res_be': jnp.zeros((D,)), 'int_W1': nrm((6 * D, D)), 'int_b1': jnp.zeros((D,)), 'int_W2': nrm((D, D)), 'int_b2': jnp.zeros((D,)), 'int_g': gamma((D,)), 'int_be': jnp.zeros((D,)), 'aw': jnp.ones((6,), jnp.float32) / 6.0}
        return inp
    _L1_cond_all = _L1_cond_setup()
    _L1_cond_in = {k: v for k, v in _L1_cond_all.items() if k in ('pw_g', 'pw_b', 'cp_g', 'cp_b', 'tm_g', 'tm_b', 'ms_g', 'ms_b', 'mem_W1', 'mem_b1', 'mem_W2', 'mem_b2', 'mem_g', 'mem_be', 'noi_W1', 'noi_b1', 'noi_W2', 'noi_b2', 'noi_g', 'noi_be', 'res_W1', 'res_b1', 'res_W2', 'res_b2', 'res_g', 'res_be', 'int_W1', 'int_b1', 'int_W2', 'int_b2', 'int_g', 'int_be', 'aw')}
    del _L1_cond_all
    return {'x': x, 'cond_512': cond_512, 'itok_BxS_0_999': itok_BxS_0_999, 'itok_BxS_0_4': itok_BxS_0_4, 'cond_64': cond_64, 'fside_Bx32_0': fside_Bx32_0, 'mask_BxS_ik0': mask_BxS_ik0, 'L0_cond_k_aff_w': _L0_cond_in['k_aff_w'], 'L0_cond_k_aff_b': _L0_cond_in['k_aff_b'], 'L0_cond_k_w': _L0_cond_in['k_w'], 'L0_cond_k_b': _L0_cond_in['k_b'], 'L0_cond_o_aff_w': _L0_cond_in['o_aff_w'], 'L0_cond_o_aff_b': _L0_cond_in['o_aff_b'], 'L0_cond_o_w': _L0_cond_in['o_w'], 'L0_cond_o_b': _L0_cond_in['o_b'], 'L1_cond_pw_g': _L1_cond_in['pw_g'], 'L1_cond_pw_b': _L1_cond_in['pw_b'], 'L1_cond_cp_g': _L1_cond_in['cp_g'], 'L1_cond_cp_b': _L1_cond_in['cp_b'], 'L1_cond_tm_g': _L1_cond_in['tm_g'], 'L1_cond_tm_b': _L1_cond_in['tm_b'], 'L1_cond_ms_g': _L1_cond_in['ms_g'], 'L1_cond_ms_b': _L1_cond_in['ms_b'], 'L1_cond_mem_W1': _L1_cond_in['mem_W1'], 'L1_cond_mem_b1': _L1_cond_in['mem_b1'], 'L1_cond_mem_W2': _L1_cond_in['mem_W2'], 'L1_cond_mem_b2': _L1_cond_in['mem_b2'], 'L1_cond_mem_g': _L1_cond_in['mem_g'], 'L1_cond_mem_be': _L1_cond_in['mem_be'], 'L1_cond_noi_W1': _L1_cond_in['noi_W1'], 'L1_cond_noi_b1': _L1_cond_in['noi_b1'], 'L1_cond_noi_W2': _L1_cond_in['noi_W2'], 'L1_cond_noi_b2': _L1_cond_in['noi_b2'], 'L1_cond_noi_g': _L1_cond_in['noi_g'], 'L1_cond_noi_be': _L1_cond_in['noi_be'], 'L1_cond_res_W1': _L1_cond_in['res_W1'], 'L1_cond_res_b1': _L1_cond_in['res_b1'], 'L1_cond_res_W2': _L1_cond_in['res_W2'], 'L1_cond_res_b2': _L1_cond_in['res_b2'], 'L1_cond_res_g': _L1_cond_in['res_g'], 'L1_cond_res_be': _L1_cond_in['res_be'], 'L1_cond_int_W1': _L1_cond_in['int_W1'], 'L1_cond_int_b1': _L1_cond_in['int_b1'], 'L1_cond_int_W2': _L1_cond_in['int_W2'], 'L1_cond_int_b2': _L1_cond_in['int_b2'], 'L1_cond_int_g': _L1_cond_in['int_g'], 'L1_cond_int_be': _L1_cond_in['int_be'], 'L1_cond_aw': _L1_cond_in['aw']}

def reference(x, cond_512, itok_BxS_0_999, itok_BxS_0_4, cond_64, fside_Bx32_0, mask_BxS_ik0, L0_cond_k_aff_w, L0_cond_k_aff_b, L0_cond_k_w, L0_cond_k_b, L0_cond_o_aff_w, L0_cond_o_aff_b, L0_cond_o_w, L0_cond_o_b, L1_cond_pw_g, L1_cond_pw_b, L1_cond_cp_g, L1_cond_cp_b, L1_cond_tm_g, L1_cond_tm_b, L1_cond_ms_g, L1_cond_ms_b, L1_cond_mem_W1, L1_cond_mem_b1, L1_cond_mem_W2, L1_cond_mem_b2, L1_cond_mem_g, L1_cond_mem_be, L1_cond_noi_W1, L1_cond_noi_b1, L1_cond_noi_W2, L1_cond_noi_b2, L1_cond_noi_g, L1_cond_noi_be, L1_cond_res_W1, L1_cond_res_b1, L1_cond_res_W2, L1_cond_res_b2, L1_cond_res_g, L1_cond_res_be, L1_cond_int_W1, L1_cond_int_b1, L1_cond_int_W2, L1_cond_int_b2, L1_cond_int_g, L1_cond_int_be, L1_cond_aw):
    import jax
    import jax.numpy as jnp

    def _L0_cond_ref(x, s, k_aff_w, k_aff_b, k_w, k_b, o_aff_w, o_aff_b, o_w, o_b):
        import jax, jax.numpy as jnp
        import numpy as np
        import math
        HEAD_NUM = 16
        EPS = 1e-08

        def modulated_linear(x, s, aff_w, aff_b, w, b):
            style = s @ aff_w.T + aff_b
            w_mod = w[None, :, :] * style[:, None, :]
            demod = jax.lax.rsqrt(jnp.sum(w_mod * w_mod, axis=2) + EPS)
            w_mod = w_mod * demod[:, :, None]
            return jnp.einsum('bni,boi->bno', x, w_mod) + b
        B, N, F = x.shape
        H = HEAD_NUM
        D = F // H
        kx = modulated_linear(x, s, k_aff_w, k_aff_b, k_w, k_b)
        kx = kx.reshape(B, N, H, D)
        q = k = v = kx
        scores = jnp.einsum('bnhd,bnjd->bnhj', q, k) / math.sqrt(D)
        A = jax.nn.softmax(scores, axis=-1)
        out = jnp.einsum('bnhj,bnjd->bnhd', A, v).reshape(B, N, F)
        out = modulated_linear(out, s, o_aff_w, o_aff_b, o_w, o_b)
        return out

    def _L1_cond_ref(x, pathway_ids, compartment_ids, time_steps, scale_type, memory_state, noise_state, resource_state, pw_g, pw_b, cp_g, cp_b, tm_g, tm_b, ms_g, ms_b, mem_W1, mem_b1, mem_W2, mem_b2, mem_g, mem_be, noi_W1, noi_b1, noi_W2, noi_b2, noi_g, noi_be, res_W1, res_b1, res_W2, res_b2, res_g, res_be, int_W1, int_b1, int_W2, int_b2, int_g, int_be, aw):
        import jax, jax.numpy as jnp
        import numpy as np
        EPS = 1e-05

        def _ln(x, g, b):
            m = jnp.mean(x, axis=-1, keepdims=True)
            v = jnp.mean((x - m) ** 2, axis=-1, keepdims=True)
            return (x - m) * jax.lax.rsqrt(v + EPS) * g + b

        def _mlp_ln(s, W1, b1, W2, b2, g, b):
            h = jax.nn.silu(s @ W1 + b1) @ W2 + b2
            return _ln(h, g, b)
        h = _ln(x, pw_g[pathway_ids], pw_b[pathway_ids])
        h = _ln(h, cp_g[compartment_ids], cp_b[compartment_ids])
        t = _ln(x, tm_g[time_steps], tm_b[time_steps])
        m = x + _mlp_ln(memory_state, mem_W1, mem_b1, mem_W2, mem_b2, mem_g, mem_be)[:, None, :]
        n = x + _mlp_ln(noise_state, noi_W1, noi_b1, noi_W2, noi_b2, noi_g, noi_be)[:, None, :]
        r = x + _mlp_ln(resource_state, res_W1, res_b1, res_W2, res_b2, res_g, res_be)[:, None, :]
        s = _ln(x, ms_g[scale_type], ms_b[scale_type])
        w = jax.nn.softmax(aw)
        cat = jnp.concatenate([w[0] * h, w[1] * t, w[2] * m, w[3] * n, w[4] * r, w[5] * s], axis=-1)
        return _mlp_ln(cat, int_W1, int_b1, int_W2, int_b2, int_g, int_be)
    x = x + _L0_cond_ref(x, cond_512, L0_cond_k_aff_w, L0_cond_k_aff_b, L0_cond_k_w, L0_cond_k_b, L0_cond_o_aff_w, L0_cond_o_aff_b, L0_cond_o_w, L0_cond_o_b)
    x = x + _L1_cond_ref(x, itok_BxS_0_999, itok_BxS_0_4, itok_BxS_0_4, mask_BxS_ik0, cond_512, cond_64, fside_Bx32_0, L1_cond_pw_g, L1_cond_pw_b, L1_cond_cp_g, L1_cond_cp_b, L1_cond_tm_g, L1_cond_tm_b, L1_cond_ms_g, L1_cond_ms_b, L1_cond_mem_W1, L1_cond_mem_b1, L1_cond_mem_W2, L1_cond_mem_b2, L1_cond_mem_g, L1_cond_mem_be, L1_cond_noi_W1, L1_cond_noi_b1, L1_cond_noi_W2, L1_cond_noi_b2, L1_cond_noi_g, L1_cond_noi_be, L1_cond_res_W1, L1_cond_res_b1, L1_cond_res_W2, L1_cond_res_b2, L1_cond_res_g, L1_cond_res_be, L1_cond_int_W1, L1_cond_int_b1, L1_cond_int_W2, L1_cond_int_b2, L1_cond_int_g, L1_cond_int_be, L1_cond_aw)
    return x

_drawn_inputs = setup_inputs


def setup_inputs(seed=0):
    import zlib

    import numpy as np

    out = dict(_drawn_inputs(seed))
    spreads = {'L0_cond_k_aff_b': (1.0, 0.2),
     'L0_cond_k_b': (0.0, 0.1),
     'L0_cond_o_aff_b': (1.0, 0.2),
     'L0_cond_o_b': (0.0, 0.1),
     'L1_cond_mem_b1': (0.0, 0.533),
     'L1_cond_mem_b2': (0.0, 0.1),
     'L1_cond_mem_be': (0.0, 0.8),
     'L1_cond_noi_b1': (0.0, 0.414),
     'L1_cond_noi_b2': (0.0, 0.1),
     'L1_cond_noi_be': (0.0, 0.8),
     'L1_cond_res_b1': (0.0, 0.445),
     'L1_cond_res_b2': (0.0, 0.1),
     'L1_cond_res_be': (0.0, 0.8),
     'L1_cond_int_b1': (0.0, 0.1),
     'L1_cond_int_b2': (0.0, 0.1),
     'L1_cond_int_be': (0.0, 0.1),
     'L1_cond_aw': (0.1666666716337204, 0.6)}
    factors = {'fside_Bx32_0': 2.703,
     'L1_cond_pw_g': 8.0,
     'L1_cond_pw_b': 8.0,
     'L1_cond_cp_g': 8.0,
     'L1_cond_cp_b': 8.0,
     'L1_cond_tm_g': 8.0,
     'L1_cond_tm_b': 8.0,
     'L1_cond_ms_g': 8.0,
     'L1_cond_ms_b': 8.0,
     'L1_cond_mem_g': 8.0,
     'L1_cond_noi_g': 8.0,
     'L1_cond_res_W1': 2.761,
     'L1_cond_res_g': 8.0,
     'L1_cond_int_g': 5.163}
    for name, (base, spread) in spreads.items():
        noise = np.random.default_rng([zlib.crc32(name.encode()), seed]).standard_normal(out[name].shape)
        drawn = base * np.exp(spread * noise) if base else spread * noise
        out[name] = jnp.asarray(drawn.astype(out[name].dtype))
    for name, factor in factors.items():
        out[name] = (out[name] * factor).astype(out[name].dtype)
    return out
```

```python
import numpy as np
import concourse.bass as bass
from concourse import mybir
from contextlib import ExitStack

F32 = mybir.dt.float32
F32R = mybir.dt.float32r
BF16 = mybir.dt.bfloat16
F16 = mybir.dt.float16
I32 = mybir.dt.int32
U32 = mybir.dt.uint32
ALU = mybir.AluOpType
ACT = mybir.ActivationFunctionType
AX = mybir.AxisListType

NG = 32
NT = 16
SCALE = 32.0 ** -0.5
NEG = -1.0e30

PROLOGUE = set("""c_eps c_L0 c_bd12 c_bd3 c_ids sty styl stsq wsq dmm dme dms dmr dn0 dn1 dn2 dmp tz rz
s3_0 s3_1 s3_2 s3_3 s3_4 s3_5 s3_6 wm ws we wd wr w6 gw vz mz m1 mh mh2 mt mhT m2 mv0 mv1 mv2 mv3 mv4
mv5 mv6 mv7 mu vT tb0 tt tabT lz lb Pm xa wh wl pb0 pbs""".split())


class Queues:

    def __init__(self):
        self.items = {e: [] for e in ("pe", "act", "dve", "pool", "sp")}
        self.count = {}
        self.value = {}
        self.owner = {}

    def put(self, eng, fn, key=None, needs=(), dma=False):
        waits = []
        for n in needs:
            if n is not None and n[1] >= 0:
                waits.append(self.value[n])
        inc = None
        if key is not None:
            step = 16 if dma else 1
            name = "pro_" + eng if key[0] in PROLOGUE else key[0]
            assert self.owner.setdefault(name, eng) == eng, key
            self.count[name] = self.count.get(name, 0) + step
            self.value[key] = (name, self.count[name])
            inc = (name, step)
        self.items[eng].append((waits, fn, inc))

    def emit(self, eng, e, sems):
        seen = {}
        for waits, fn, inc in self.items[eng]:
            for stage, v in waits:
                if seen.get(stage, 0) < v:
                    e.wait_ge(sems[stage], v)
                    seen[stage] = v
            if fn is None:
                continue
            i = fn(e)
            if inc:
                i.then_inc(sems[inc[0]], inc[1])


def build(nc, A, out):
    Q = Queues()
    put = Q.put
    ctx = ExitStack()
    with ctx:
        def sb(name, shape, dt=F32, c=ctx):
            return c.enter_context(nc.sbuf_tensor(name, shape, dt))

        ident = sb("ident", [128, 128])
        cst = sb("cst", [128, 5])
        selT = sb("selT", [128, 3, 128], BF16)
        maskL = sb("maskL", [128, 128], BF16)
        maskR = sb("maskR", [128, 32], BF16)
        gint = sb("gint", [128, 512])
        beint = sb("beint", [128, 512])
        biasT = sb("biasT", [128, 512], BF16)
        GT = {n: sb("G" + n, [128, 512], BF16) for n in "ths"}
        PT = sb("PT", [128, 512], BF16)
        w6 = sb("w6", [128, 6])
        styl = sb("styl", [128, 2, 4, 4])
        pidx = sb("pidx", [128, NG], I32)
        W1 = {(n, p): sb(f"W1{n}{p}", [128, 4, 512], F32R) for n in "xtsh" for p in "hl"}
        WL = {(n, p): sb(f"W{n}{p}", [128, 4, 512], F32R) for n in ("k", "o", "2") for p in "hl"}
        NRING = 2
        ring = [sb(f"ring{i}", [128, 512]) for i in range(NRING)]
        ytmp = [sb(f"ytmp{i}", [128, 512]) for i in range(2)]
        small = sb("small", [128, 96])
        eps5 = small[:, 0:1]
        mh = cst[:, 4:5]

        ids = sb("ids", [128, 256], I32)
        OH = [sb(f"OH{i}", [128, 256], BF16) for i in range(2)]
        xraw = sb("xraw", [128, 4, 128])
        xhi = sb("xhi", [128, 4, 128], F32R)
        xlo = sb("xlo", [128, 4, 128], F32R)
        q = sb("q", [128, 512])
        q12 = sb("q12", [128, 512, 2], BF16)
        q3 = sb("q3", [128, 512], BF16)
        v12 = sb("v12", [128, 512, 2], BF16)
        v3 = sb("v3", [128, 512], BF16)
        BD12 = sb("BD12", [128, 16, 4, 32, 2], BF16)
        BD3 = sb("BD3", [128, 16, 4, 32], BF16)
        SE = sb("SE", [128, 512])
        ET = sb("ET", [128, 512])
        e12 = sb("e12", [128, 512, 2], F16)
        ahi = sb("ahi", [128, 4, 128], F32R)
        alo = sb("alo", [128, 4, 128], F32R)
        xb = [sb(f"xb{i}", [128, 512]) for i in range(4)]
        dramtmp = nc.dram_tensor("dmscratch", (2, 4, 512), F32, kind="Internal").ap()
        ps = {n: ctx.enter_context(nc.psum_tensor(n, [128, 512], F32))
              for n in ("acc0", "acc1", "tok0", "tok1", "att0", "att1", "xp0", "xp1")}
        main = ExitStack()
        pro = ExitStack()
        with pro:
            psb = lambda n, s, d=F32: sb(n, s, d, pro)
            P = dict(
                h=psb("p_h", [128, 512]), hT=psb("p_hT", [128, 4, 128]),
                L0=psb("p_L0", [128, 4, 96]), L1=psb("p_L1", [128, 4, 96]),
                t0=psb("p_t0", [128, 512]), t1=psb("p_t1", [128, 512]), t2=psb("p_t2", [128, 512]),
                tabT=psb("p_tabT", [128, 4, 128]),
                condT=psb("p_condT", [128, 4, 4]), abc=psb("p_abc", [128, 2, 4]),
                aw=psb("p_aw", [128, 6]), st2=psb("p_st2", [128, 2, 4, 4]),
                dmr=psb("p_dmr", [128, 2]),
            )
        ctx.enter_context(main)
        msb = lambda n, s, d=F32: sb(n, s, d, main)
        op = [{p: msb(f"op{i}{p}", [128, 4, 256], F32R) for p in "hl"} for i in range(2)]
        zT = msb("zT", [128, 4, 256])
        uT = msb("uT", [128, 4, 128])
        z = sb("z", [128, 512])
        pgb = sb("pgb", [128, 1024])
        dmb = sb("dmb", [128, 512])

        tok_n = [0]
        tok_free = [(), ()]
        xp_n = [0]
        xp_free = [(), ()]

        def tok_bank():
            s = tok_n[0] % 2
            tok_n[0] += 1
            return s, ps[f"tok{s}"], tok_free[s]

        def xp_bank():
            s = xp_n[0] % 2
            xp_n[0] += 1
            return s, ps[f"xp{s}"], xp_free[s]

        y_n = [0]
        y_free = [(), ()]

        def y_buf():
            s = y_n[0] % 2
            y_n[0] += 1
            return s, ytmp[s], y_free[s]

        r_n = [0]
        r_free = [()] * NRING

        def load_chunk(src):
            s = r_n[0] % NRING
            n = r_n[0]
            r_n[0] += 1
            key = (f"ring{s}", n)
            put("sp", lambda e: e.dma_start(ring[s][:, :], src), key, r_free[s], dma=True)
            return s, ring[s], key

        def mm(e, o, a, b, start=False):
            return e.matmul(o, a, b, start=start, stop=True, skip_group_check=True)

        def three(e, o, ah, al, bh, bl, start):
            mm(e, o, ah, bh, start)
            mm(e, o, ah, bl)
            return mm(e, o, al, bh)

        def consts():
            put("sp", lambda e: e.dma_start(P["condT"][:, :, :], A["condT"]), ("c_cond", 0), dma=True)
            put("sp", lambda e: e.dma_start(P["abc"][:, :, :], A["affb"]), ("c_abc", 0), dma=True)
            put("sp", lambda e: e.dma_start(cst[:, :], A["cst"]), ("c_cst", 0), dma=True)
            put("act", lambda e: e.dma_start(ident[:, :], A["ident"]), ("c_id", 0), dma=True)
            put("act", lambda e: e.dma_start(selT[:, :, :], A["selT"]), ("c_sel", 0), dma=True)
            put("act", lambda e: e.dma_start(maskL[:, :], A["maskL"]), ("c_mL", 0), dma=True)
            put("act", lambda e: e.dma_start(maskR[:, :], A["maskR"]), ("c_mR", 0), dma=True)
            put("act", lambda e: e.dma_start(pidx[:, :], A["pidx"]), ("c_pidx", 0), dma=True)
            put("act", lambda e: e.dma_start(P["aw"][:, :], A["aw"].partition_broadcast(128)), ("c_aw", 0), dma=True)
            put("act", lambda e: e.dma_start(gint[:, :], A["int_g"].partition_broadcast(128)), ("c_gi", 0), dma=True)
            put("act", lambda e: e.dma_start(beint[:, :], A["int_be"].partition_broadcast(128)), ("c_be", 0), dma=True)
            put("dve", lambda e: e.memset(eps5, 1e-5), ("c_eps", 0))
            put("dve", lambda e: e.memset(P["L0"][:, :, :], 0.0), ("c_L0", 0))
            put("pool", lambda e: e.memset(BD12[:, :, :, :, :].bitcast(U32), 0), ("c_bd12", 0))
            put("pool", lambda e: e.memset(BD3[:, :, :, :].bitcast(U32), 0), ("c_bd3", 0))
            put("pool", lambda e: e.memset(ids[:, :], 0), ("c_ids", 0))

        def split3(src, dst, tag, needs):
            a, b = P["t1"], P["t2"]
            p1, p2 = b[:, 0:256].bitcast(BF16), b[:, 256:512].bitcast(BF16)
            k = lambda i: (f"s3_{i}", tag)
            put("dve", lambda e: e.tensor_copy(p1, src), k(0), list(needs) + [("s3_5", tag - 1), ("dmst0", 0), ("dmst1", 0)])
            put("dve", lambda e: e.tensor_tensor(src, src, p1, ALU.subtract), k(1), [k(0)])
            put("dve", lambda e: e.tensor_scalar(a[:, :], p1, cst[:, 1:2], None, ALU.mult), k(2), [k(0), ("c_cst", 0), ("s3_6", tag - 1)])
            put("dve", lambda e: e.tensor_copy(p2, src), k(3), [k(1)])
            put("dve", lambda e: e.tensor_tensor(src, src, p2, ALU.subtract), k(4), [k(3)])
            put("dve", lambda e: e.scalar_tensor_tensor(out=a[:, :], in0=p2, scalar=cst[:, 2:3], in1=a[:, :], op0=ALU.mult, op1=ALU.add), k(5), [k(2), k(3)])
            put("dve", lambda e: e.scalar_tensor_tensor(out=dst, in0=src, scalar=cst[:, 3:4], in1=a[:, :], op0=ALU.mult, op1=ALU.add), k(6), [k(4), k(5)])

        def rows_in(t, tag, rows, free):
            put("dve", lambda e: e.memset(t[:, :], 0.0), ("rz", tag), free)
            for i, (r, n, src) in enumerate(rows):
                for rep in range(3):
                    put("sp", lambda e, r=r, n=n, src=src, rep=rep: e.dma_start(t[r + 8 * rep:r + 8 * rep + n, :], src),
                        ("rows", tag * 100 + i * 3 + rep), [("rz", tag)], dma=True)
            return ("rows", tag * 100 + 3 * len(rows) - 1)

        def bias_table():
            k = rows_in(P["t0"], 0, [(0, 1, A["kb"]), (32, 1, A["ob"]), (64, 1, A["b2"])], [("dn1", 1)])
            split3(P["t0"][:, :], biasT[:, :], 0, [k])

        def g_tables():
            for n, (name, w, tab, r, nr) in enumerate((("t", 1, "tm_g", 0, 5), ("s", 5, "ms_g", 32, 3), ("h", 0, "cp_g", 0, 5))):
                k = rows_in(P["t0"], 1 + n, [(r, nr, A[tab])], [("s3_6", n)])
                put("dve", lambda e, w=w: e.tensor_scalar(P["t0"][:, :], P["t0"][:, :], w6[:, w:w + 1], None, ALU.mult),
                    ("gw", n), [k, ("w6", 0)])
                split3(P["t0"][:, :], GT[name][:, :], 1 + n, [("gw", n)])

        def weights_softmax():
            aw = P["aw"]
            put("dve", lambda e: e.tensor_reduce(small[:, 1:2], aw[:, :], axis=AX.X, op=ALU.max), ("wm", 0), [("c_aw", 0)])
            put("dve", lambda e: e.tensor_scalar(aw[:, :], aw[:, :], small[:, 1:2], None, ALU.subtract), ("ws", 0), [("wm", 0)])
            put("act", lambda e: e.activation(aw[:, :], aw[:, :], ACT.Exp), ("we", 0), [("ws", 0)])
            put("dve", lambda e: e.tensor_reduce(small[:, 2:3], aw[:, :], axis=AX.X, op=ALU.add), ("wd", 0), [("we", 0)])
            put("dve", lambda e: e.reciprocal(small[:, 3:4], small[:, 2:3]), ("wr", 0), [("wd", 0)])
            put("dve", lambda e: e.tensor_scalar(w6[:, :], aw[:, :], small[:, 3:4], None, ALU.mult), ("w6", 0), [("wr", 0)])

        def styles():
            for L, nm in enumerate(("k", "o")):
                slots = []
                for st in range(2):
                    slots.append(load_chunk(A[nm + "_affT"][st]))
                s, bank, free = xp_bank()
                for kt in range(4):
                    for st in range(2):
                        last = kt == 3 and st == 1
                        put("pe", lambda e, kt=kt, st=st, c=slots[st][1], bank=bank: mm(
                            e, bank[:, kt * 4:kt * 4 + 4], c[:, kt * 128:kt * 128 + 128], P["condT"][:, st, :], start=(kt == 0 and st == 0)),
                            ("sty", L) if last else None, [slots[st][2], ("c_cond", 0), *free])
                for st in range(2):
                    r_free[slots[st][0]] = (("sty", L),)
                put("dve", lambda e, L=L, bank=bank: e.tensor_tensor(
                    styl[:, L, :, :], bank[:, 0:16].rearrange("p (k b) -> p k b", b=4),
                    P["abc"][:, L, :].unsqueeze(2).to_broadcast([128, 4, 4]), ALU.add), ("styl", L), [("sty", L), ("c_abc", 0)])
                xp_free[s] = (("styl", L),)
                put("dve", lambda e, L=L: e.tensor_tensor(P["st2"][:, L, :, :], styl[:, L, :, :], styl[:, L, :, :], ALU.mult), ("stsq", L), [("styl", L)])
            for L, nm in enumerate(("k", "o")):
                s, bank, free = xp_bank()
                for kt in range(4):
                    cs, c, key = load_chunk(A[nm + "_wT"][kt])
                    ys, y, yf = y_buf()
                    put("act", lambda e, c=c, y=y: e.activation(y[:, :], c[:, :], ACT.Square), ("wsq", L * 4 + kt), [key, *yf])
                    r_free[cs] = (("wsq", L * 4 + kt),)
                    put("pe", lambda e, y=y, L=L, kt=kt, bank=bank: mm(e, bank[0:4, :], P["st2"][:, L, kt, :], y[:, :], start=(kt == 0)),
                        ("dmm", L * 4 + kt), [("wsq", L * 4 + kt), ("stsq", L), *free])
                    y_free[ys] = (("dmm", L * 4 + kt),)
                t = P["t1"] if L == 0 else P["t2"]
                put("dve", lambda e, bank=bank: e.tensor_scalar(P["t0"][0:4, :], bank[0:4, :], 1e-8, None, ALU.add), ("dme", L), [("dmm", L * 4 + 3), ("dn1", L - 1)])
                xp_free[s] = (("dme", L),)
                put("act", lambda e, t=t: e.activation(t[0:4, :], P["t0"][0:4, :], ACT.Sqrt), ("dms", L), [("dme", L)])
                v, y, u = P["t0"][0:4, :], t[0:4, :], P["h"][0:4, :]
                put("dve", lambda e, y=y: e.reciprocal(y, y), ("dmr", L), [("dms", L)])
                put("dve", lambda e, y=y: e.tensor_tensor(u, y, y, ALU.mult), ("dn0", L), [("dmr", L)])
                put("dve", lambda e: e.tensor_tensor(u, u, v, ALU.mult), ("dn1", L), [("dn0", L)])
                put("dve", lambda e: e.tensor_scalar(u, u, -0.5, 1.5, ALU.mult, ALU.add), ("dn2", L), [("dn1", L)])
                put("dve", lambda e, y=y: e.tensor_tensor(y, y, u, ALU.mult), ("dmp", L), [("dn2", L)])
                put("sp", lambda e, L=L, t=t: e.dma_start(dramtmp[L], t[0:4, :]), (f"dmst{L}", 0), [("dmp", L)], dma=True)

        def mod_weights(b, L):
            nm = "ko"[L]
            n = b * 2 + L
            last_use = ("A", 8 * b - 1) if L == 0 else ("O", 8 * b - 1)
            put("sp", lambda e: e.dma_start(dmb[:, :], dramtmp[L, b, :].partition_broadcast(128)), ("dmb", n),
                [("dmst0", 0), ("dmst1", 0), ("stt", 4 * n - 1)], dma=True)
            for kt in range(4):
                cs, c, key = load_chunk(A[nm + "_wT"][kt])
                ys, y, yf = y_buf()
                i = 4 * n + kt
                put("dve", lambda e, c=c, y=y, kt=kt: e.scalar_tensor_tensor(
                    out=y[:, :], in0=c[:, :], scalar=styl[:, L, kt, b:b + 1], in1=dmb[:, :], op0=ALU.mult, op1=ALU.mult),
                    ("stt", i), [key, ("dmb", n), ("styl", L), *yf])
                r_free[cs] = (("stt", i),)
                put("act", lambda e, y=y, kt=kt: e.copy(WL[nm, "h"][:, kt, :], y[:, :]), ("mwh", i), [("stt", i), last_use])
                put("dve", lambda e, y=y, kt=kt: e.tensor_tensor(WL[nm, "l"][:, kt, :], y[:, :], WL[nm, "h"][:, kt, :].bitcast(F32), ALU.subtract),
                    ("mwl", i), [("mwh", i), last_use])
                y_free[ys] = (("mwl", i),)
            mw_done[b, L] = [("mwh", 4 * n + 3), ("mwl", 4 * n + 3)]

        mw_done = {}
        nw = [0]

        def split_weight(y, ykeys, H, Lo, kt):
            i = nw[0]
            nw[0] += 1
            put("act", lambda e: e.copy(H[:, kt, :], y[:, :]), ("wh", i), ykeys)
            put("pool", lambda e: e.tensor_tensor(Lo[:, kt, :], y[:, :], H[:, kt, :].bitcast(F32), ALU.subtract), ("wl", i), [("wh", i)])
            return (("wh", i), ("wl", i))

        def w2_weights():
            for kt in range(4):
                cs, c, key = load_chunk(A["int_w2"][kt])
                rd = split_weight(c, [key], WL["2", "h"], WL["2", "l"], kt)
                r_free[cs] = rd
                w2_done[0] = list(rd)

        w2_done = [None]

        nets = [("mem", 0, (0, 1)), ("noi", 32, (2,)), ("res", 64, (3,))]

        def mlp():
            h, hT, t0, t1 = P["h"], P["hT"], P["t0"], P["t1"]
            tfree = [("s3_6", 3)]

            def vec_rows(tag, t, name, free):
                put("dve", lambda e: e.memset(t[:, :], 0.0), ("vz", tag), free)
                for i, (n, r, _) in enumerate(nets):
                    put("sp", lambda e, r=r, n=n: e.dma_start(t[r:r + 4, :], A[n + name].partition_broadcast(4)), (f"vr{tag}", i), [("vz", tag)], dma=True)
                return (f"vr{tag}", 2)

            kb1 = vec_rows(0, t0, "_b1", tfree)
            kb2 = vec_rows(1, t1, "_b2", tfree)
            kg = vec_rows(2, P["t2"], "_g", tfree)
            s, bank, free = xp_bank()
            put("pe", lambda e, bank=bank: mm(e, bank[:, :], P["tabT"][:, 0, :], P["tabT"][:, :, :].rearrange("p a b -> p (a b)"), start=True), ("mz", 0), [("tz", 0), *free])
            for i, (n, r, cs_) in enumerate(nets):
                for j, ci in enumerate(cs_):
                    sl, c, key = load_chunk(A[n + "_w1"][j])
                    put("pe", lambda e, r=r, ci=ci, c=c, bank=bank: mm(e, bank[r:r + 4, :], P["condT"][:, ci, :], c[:, :]),
                        ("m1", i * 2 + j), [key])
                    r_free[sl] = (("m1", i * 2 + j),)
            put("dve", lambda e, bank=bank: e.tensor_tensor(h[:, :], bank[:, :], t0[:, :], ALU.add), ("mh", 0), [("m1", 4), kb1])
            xp_free[s] = (("mh", 0),)
            kbe = vec_rows(3, t0, "_be", [("mh", 0)])
            put("act", lambda e: e.activation(h[:, :], h[:, :], ACT.Silu), ("mh2", 0), [("mh", 0)])
            s, bank, free = xp_bank()
            for kt in range(4):
                put("pe", lambda e, kt=kt, bank=bank: e.transpose(bank[:, kt * 128:kt * 128 + 128], h[:, kt * 128:kt * 128 + 128], ident[:, :]),
                    ("mt", kt), [("mh2", 0), ("c_id", 0), *free])
            put("dve", lambda e, bank=bank: e.tensor_copy(hT[:, :, :].rearrange("p a b -> p (a b)"), bank[:, :]), ("mhT", 0), [("mt", 3)])
            xp_free[s] = (("mhT", 0),)
            s, bank, free = xp_bank()
            put("pe", lambda e, bank=bank: mm(e, bank[:, :], P["tabT"][:, 0, :], P["tabT"][:, :, :].rearrange("p a b -> p (a b)"), start=True), ("mz", 1), [*free])
            for i, (n, r, _) in enumerate(nets):
                for kt in range(4):
                    sl, c, key = load_chunk(A[n + "_w2"][kt])
                    put("pe", lambda e, r=r, kt=kt, c=c, bank=bank: mm(e, bank[r:r + 4, :], hT[:, kt, r:r + 4], c[:, :]),
                        ("m2", i * 4 + kt), [key, ("mhT", 0)])
                    r_free[sl] = (("m2", i * 4 + kt),)
            put("dve", lambda e, bank=bank: e.tensor_tensor(h[:, :], bank[:, :], t1[:, :], ALU.add), ("mv0", 0), [("m2", 11), kb2, ("mt", 3)])
            xp_free[s] = (("mv0", 0),)
            bs = small[:, 8:14]
            mv = small[:, 14:16]
            put("dve", lambda e: e.bn_stats(bs, h[:, :]), ("mv1", 0), [("mv0", 0)])
            put("dve", lambda e: e.bn_aggr(mv, bs), ("mv2", 0), [("mv1", 0)])
            put("pool", lambda e: e.tensor_tensor(small[:, 16:17], mv[:, 1:2], eps5, ALU.add), ("mv3", 0), [("mv2", 0), ("c_eps", 0)])
            put("pool", lambda e: e.tensor_tensor(small[:, 17:18], small[:, 16:17], mh, ALU.pow), ("mv4", 0), [("mv3", 0), ("c_cst", 0)])
            put("dve", lambda e: e.tensor_scalar(h[:, :], h[:, :], mv[:, 0:1], small[:, 17:18], ALU.subtract, ALU.mult), ("mv5", 0), [("mv4", 0)])
            put("dve", lambda e: e.tensor_tensor(h[:, :], h[:, :], P["t2"][:, :], ALU.mult), ("mv6", 0), [("mv5", 0), kg])
            put("dve", lambda e: e.tensor_tensor(h[:, :], h[:, :], t0[:, :], ALU.add), ("mv7", 0), [("mv6", 0), kbe])
            s, bank, free = xp_bank()
            for kt in range(4):
                put("pe", lambda e, kt=kt, bank=bank: e.transpose(bank[:, kt * 128:kt * 128 + 128], h[:, kt * 128:kt * 128 + 128], ident[:, :]),
                    ("mu", kt), [("mv7", 0), *free])
            put("dve", lambda e, bank=bank: e.tensor_copy(hT[:, :, :].rearrange("p a b -> p (a b)"), bank[:, :]), ("vT", 0), [("mu", 3), ("m2", 11)])
            xp_free[s] = (("vT", 0),)

        def table_T():
            t, tabT = P["t1"], P["tabT"]
            put("dve", lambda e: e.memset(t[:, :], 0.0), ("tb0", 0), [("mv0", 0)])
            for i, (r, n, name) in enumerate(((0, 5, "cp_b"), (32, 5, "tm_b"), (64, 3, "ms_b"))):
                put("sp", lambda e, r=r, n=n, name=name: e.dma_start(t[r:r + n, :], A[name]), ("tb", i), [("tb0", 0)], dma=True)
            s, bank, free = xp_bank()
            for kt in range(4):
                put("pe", lambda e, kt=kt, bank=bank: e.transpose(bank[:, kt * 128:kt * 128 + 128], t[:, kt * 128:kt * 128 + 128], ident[:, :]),
                    ("tt", kt), [("tb", 2), *free])
            put("dve", lambda e, bank=bank: e.tensor_copy(tabT[:, :, :].rearrange("p a b -> p (a b)"), bank[:, :]), ("tabT", 0), [("tt", 3), ("mz", 1)])
            xp_free[s] = (("tabT", 0),)

        def w1_and_P():
            spec = [("m", 2, "hT", 0, 4, 64), ("n", 3, "hT", 32, 4, 64), ("r", 4, "hT", 64, 4, 64),
                    ("t", 1, "tabT", 32, 5, 0), ("s", 5, "tabT", 64, 3, 32), ("h", 0, "tabT", 0, 5, 0)]
            Pp = ps["acc0"]
            xacc = P["h"]
            blk = {"h": 0, "t": 1, "m": 2, "n": 3, "r": 4, "s": 5}

            L2 = P["t2"]
            LB3 = [P["L0"][:, :, :], P["L1"][:, :, :], L2[:, 0:384].rearrange("p (a b) -> p a b", b=96)]
            for j in range(3):
                name, w, src, c0, n, base = spec[j]
                t = LB3[j]
                put("dve", lambda e, t=t: e.memset(t, 0.0), ("lz", j), [("mv6", 0), ("c_L0", 0)])
                for rep in range(3):
                    put("dve", lambda e, rep=rep, t=t, w=w, c0=c0, src=src: e.tensor_scalar(t[:, :, 64 + 8 * rep:68 + 8 * rep], hT_(src)[:, :, c0:c0 + 4], w6[:, w:w + 1], None, ALU.mult),
                        ("lb", 3 * j + rep), [("lz", j), ("w6", 0), ("vT", 0)])
            for kt in range(4):
                for j in range(3):
                    name, w = spec[j][:2]
                    sl, c, key = load_chunk(A["int_w1"][blk[name] * 4 + kt])
                    first = kt == 0 and j == 0
                    put("pe", lambda e, j=j, kt=kt, c=c, first=first: mm(e, Pp[0:96, :], LB3[j][:, kt, :], c[:, :], start=first),
                        ("Pm", kt * 3 + j), [key, ("lb", 3 * j + 2)])
                    if j == 0:
                        put("dve", lambda e, c=c: e.tensor_scalar(xacc[:, :], c[:, :], w6[:, 2:3], None, ALU.mult), ("xa", 3 * kt), [key, ("mu", 3), *xfree[0]])
                    else:
                        put("dve", lambda e, c=c, w=w: e.scalar_tensor_tensor(out=xacc[:, :], in0=c[:, :], scalar=w6[:, w:w + 1], in1=xacc[:, :], op0=ALU.mult, op1=ALU.add),
                            ("xa", 3 * kt + j), [key, ("xa", 3 * kt + j - 1)])
                    r_free[sl] = (("Pm", kt * 3 + j), ("xa", 3 * kt + j))
                xfree[0] = split_weight(xacc, [("xa", 3 * kt + 2)], W1["x", "h"], W1["x", "l"], kt)
            w1_done["x"] = list(xfree[0])
            for j in range(3, 6):
                name, w, src, c0, n, base = spec[j]
                t = LB3[j - 3]
                put("dve", lambda e, t=t: e.memset(t, 0.0), ("lz", j), [("Pm", 9 + j - 3)])
                for rep in range(3):
                    put("dve", lambda e, rep=rep, t=t, w=w, c0=c0, n=n, base=base, src=src: e.tensor_scalar(
                        t[:, :, base + 8 * rep:base + n + 8 * rep], hT_(src)[:, :, c0:c0 + n], w6[:, w:w + 1], None, ALU.mult),
                        ("lb", 3 * j + rep), [("lz", j), ("tabT", 0)])
                for kt in range(4):
                    sl, c, key = load_chunk(A["int_w1"][blk[name] * 4 + kt])
                    put("pe", lambda e, t=t, kt=kt, c=c: mm(e, Pp[0:96, :], t[:, kt, :], c[:, :]), ("Pm", 12 + (j - 3) * 4 + kt), [key, ("lb", 3 * j + 2)])
                    rd = split_weight(c, [key], W1[name, "h"], W1[name, "l"], kt)
                    r_free[sl] = (("Pm", 12 + (j - 3) * 4 + kt), *rd)
                    w1_done[name] = list(rd)
            t0 = P["t0"]
            put("dve", lambda e: e.memset(t0[:, :], 0.0), ("pb0", 0), [("mv7", 0)])
            for rep in range(3):
                put("sp", lambda e, rep=rep: e.dma_start(t0[64 + 8 * rep:68 + 8 * rep, :], A["int_b1"].partition_broadcast(4)), ("pb", rep), [("pb0", 0)], dma=True)
            put("dve", lambda e: e.tensor_tensor(t0[0:96, :], t0[0:96, :], Pp[0:96, :], ALU.add), ("pbs", 0), [("pb", 2), ("Pm", 23)])
            split3(t0[:, :], PT[:, :], 4, [("pbs", 0), ("Pm", 23), ("tt", 3)])

        xfree = [()]
        w1_done = {}

        def hT_(src):
            return P[src]

        def load_x(g):
            put("sp", lambda e: e.dma_start(xraw[:, :, :], A["xT"][g]), ("ldx", g), [("xlo", g - 1), ("xhi", g - 1)], dma=True)

        def load_tok(g):
            s = g % 4
            put("sp", lambda e: e.dma_start(xb[s][:, :], A["x"][g * 128:g * 128 + 128, :]), (f"ldt{s}", g), [(f"out{s}", g - 4)], dma=True)

        def split_x(g):
            put("act", lambda e: e.copy(xhi[:, :, :], xraw[:, :, :]), ("xhi", g), [("ldx", g), ("A", g - 1)])
            put("pool", lambda e: e.tensor_tensor(xlo[:, :, :], xraw[:, :, :], xhi[:, :, :].bitcast(F32), ALU.subtract), ("xlo", g), [("xhi", g), ("ldx", g), ("A", g - 1)])

        qslot = {}

        def stage_A(g):
            s, bank, free = tok_bank()
            b = g // 8
            for kt in range(4):
                put("pe", lambda e, kt=kt: three(e, bank[:, :], xhi[:, kt, :], xlo[:, kt, :], WL["k", "h"][:, kt, :], WL["k", "l"][:, kt, :], kt == 0),
                    None, [("xhi", g), ("xlo", g), *mw_done[b, 0], *free])
            put("pe", lambda e: mm(e, bank[:, :], selT[:, 0, :], biasT[:, :]), ("A", g), [("c_sel", 0), ("s3_6", 0)])
            put("dve", lambda e: e.transpose(q[:, :].rearrange("p (t h) -> p h t", h=16), bank[:, :].rearrange("p (h t) -> p h t", h=16)),
                ("qT", g), [("A", g), ("q3", g - 1), ("q2", g - 1)])
            tok_free[s] = (("qT", g),)
            used = [("S", g - 1), ("VT", g - 1), ("bdq", g - 1)]
            put("act", lambda e: e.copy(q12[:, :, 0], q[:, :]), ("q1", g), [("qT", g), *used])
            put("pool", lambda e: e.tensor_tensor(q[:, :], q[:, :], q12[:, :, 0], ALU.subtract), ("qr", g), [("q1", g), ("qT", g)])
            put("act", lambda e: e.copy(q12[:, :, 1], q[:, :]), ("q2", g), [("qr", g), *used])
            put("pool", lambda e: e.tensor_tensor(q3[:, :], q[:, :], q12[:, :, 1], ALU.subtract), ("q3", g), [("q2", g), ("S", g - 1), ("VT3", g - 1), ("bdq3", g - 1)])

        def stage_bdq(g):
            for i in range(4):
                r = slice(32 * i, 32 * i + 32)
                put("dve", lambda e, i=i, r=r: e.tensor_copy(BD12[r, :, i, :, :].rearrange("p g m t -> p g (m t)"), q12[r, :, :].rearrange("p (g m) t -> p g (m t)", g=16)),
                    ("bdq", g) if i == 3 else None, [("q1", g), ("q2", g), ("AV", g - 1), ("c_bd12", 0)])
            for i in range(4):
                r = slice(32 * i, 32 * i + 32)
                put("act", lambda e, i=i, r=r: e.copy(BD3[r, :, i, :], q3[r, :].rearrange("p (g m) -> p g m", g=16)),
                    ("bdq3", g) if i == 3 else None, [("q3", g), ("S", g - 1), ("c_bd3", 0)])

        def stage_V(g):
            put("dve", lambda e: e.transpose(v12[:, :, :].rearrange("p a b -> p (a b)").bitcast(U32), q12[:, :, :].rearrange("p a b -> p (a b)").bitcast(U32)),
                ("VT", g), [("q1", g), ("q2", g), ("AV", g - 1)])
            put("dve", lambda e: e.transpose(v3[:, :], q3[:, :]), ("VT3", g), [("q3", g), ("AV", g - 1)])

        def stage_S(g):
            att = ps["att0"]

            def run(e, j):
                c = slice(j * 32, j * 32 + 32)
                o = att[:, c]
                w1 = BD12[:, j, :, :, 0].rearrange("p a b -> p (a b)")
                w2 = BD12[:, j, :, :, 1].rearrange("p a b -> p (a b)")
                w3 = BD3[:, j, :, :].rearrange("p a b -> p (a b)")
                r1, r2, r3 = q12[:, c, 0], q12[:, c, 1], q3[:, c]
                for a, b in ((w1, r1), (w1, r2), (w1, r3), (w2, r1), (w2, r2)):
                    mm(e, o, a, b)
                return mm(e, o, w3, r1)

            put("pe", lambda e: mm(e, att[:, :], maskL[:, :], maskR[:, :].unsqueeze(1).to_broadcast([128, 16, 32]), start=True), None,
                [("sub", g - 1), ("c_mL", 0), ("c_mR", 0)])
            for j in range(16):
                put("pe", lambda e, j=j: run(e, j), ("S", g) if j == 15 else None, [("bdq", g), ("bdq3", g), ("q3", g)])
            v = lambda t: t[:, :].rearrange("p (g m) -> p g m", m=32)
            mx, den, rden = small[:, 18:34], small[:, 34:50], small[:, 50:66]
            put("dve", lambda e: e.tensor_reduce(mx, v(att), axis=AX.X, op=ALU.max), ("mx", g), [("S", g), ("sub", g - 1)])
            put("dve", lambda e: e.tensor_tensor(v(SE), v(att), mx.unsqueeze(2).to_broadcast([128, 16, 32]), ALU.subtract),
                ("sub", g), [("mx", g), ("aTr", g - 1)])
            put("act", lambda e: e.activation(SE[:, :], SE[:, :], ACT.Exp, scale=SCALE), ("exp", g), [("sub", g)])
            put("dve", lambda e: e.transpose(ET[:, :], SE[:, :]), ("ET", g), [("exp", g), ("nT2", g - 1)])
            put("act", lambda e: e.copy(e12[:, :, 0], ET[:, :]), ("e1", g), [("ET", g), ("bde", g - 1)])
            put("dve", lambda e: e.tensor_reduce(den, v(SE), axis=AX.X, op=ALU.add), ("den", g), [("exp", g)])
            put("dve", lambda e: e.tensor_tensor(e12[:, :, 1], ET[:, :], e12[:, :, 0], ALU.subtract), ("e2", g), [("e1", g), ("ET", g), ("bde", g - 1)])
            put("dve", lambda e: e.reciprocal(rden, den), ("rden", g), [("den", g), ("norm", g - 1)])
            for i in range(4):
                r = slice(32 * i, 32 * i + 32)
                put("dve", lambda e, i=i, r=r: e.tensor_copy(BD12[r, :, i, :, :].rearrange("p g m t -> p g (m t)").bitcast(F16), e12[r, :, :].rearrange("p (g m) t -> p g (m t)", g=16)),
                    ("bde", g) if i == 3 else None, [("e1", g), ("e2", g), ("S", g)])

        def stage_AV(g):
            att = ps["att1"]

            def run(e, j):
                c = slice(j * 32, j * 32 + 32)
                o = att[:, c]
                w1 = BD12[:, j, :, :, 0].rearrange("p a b -> p (a b)").bitcast(F16)
                w2 = BD12[:, j, :, :, 1].rearrange("p a b -> p (a b)").bitcast(F16)
                mm(e, o, w1, v12[:, c, 0], start=(j == 0))
                mm(e, o, w1, v12[:, c, 1])
                mm(e, o, w1, v3[:, c])
                mm(e, o, w2, v12[:, c, 0])
                return mm(e, o, w2, v12[:, c, 1])

            for j in range(16):
                put("pe", lambda e, j=j: run(e, j), ("AV", g) if j == 15 else None, [("bde", g), ("VT", g), ("VT3", g), ("norm", g - 1)])
            rden = small[:, 50:66]
            v = lambda t: t[:, :].rearrange("p (g m) -> p g m", m=32)
            put("dve", lambda e: e.tensor_tensor(v(SE), v(att), rden.unsqueeze(2).to_broadcast([128, 16, 32]), ALU.mult), ("norm", g), [("AV", g), ("rden", g), ("den", g), ("ET", g)])
            put("dve", lambda e: e.transpose(ET[:, :].rearrange("p (h g t) -> p g t h", h=16, t=2), SE[:, :]), ("nT", g), [("norm", g), ("e1", g), ("e2", g)])
            put("dve", lambda e: e.transpose(SE[:, :], ET[:, :]), ("nT2", g), [("nT", g)])

        def stage_aTr(g):
            s, bank, free = xp_bank()
            for c in range(4):
                put("pe", lambda e, c=c: e.transpose(bank[:, c * 128:c * 128 + 128], SE[:, c * 128:c * 128 + 128], ident[:, :]),
                    ("aTr", g) if c == 3 else None, [("nT2", g), ("c_id", 0), *free])
            v = bank[:, :].rearrange("p (c t) -> p c t", c=4)
            put("act", lambda e: e.copy(ahi[:, :, :], v), ("ahi", g), [("aTr", g), ("O", g - 1)])
            put("dve", lambda e: e.tensor_tensor(alo[:, :, :], v, ahi[:, :, :].bitcast(F32), ALU.subtract), ("alo", g), [("ahi", g), ("O", g - 1)])
            xp_free[s] = (("alo", g),)

        st1, mv1, rs1 = small[:, 66:72], small[:, 72:74], small[:, 74:76]
        st2_, mv2, rs2 = small[:, 76:82], small[:, 82:84], small[:, 84:86]
        st3, mv3, rs3 = small[:, 86:92], small[:, 92:94], small[:, 94:96]

        def stage_O(g):
            s, bank, free = tok_bank()
            b = g // 8
            xs = xb[g % 4]
            for kt in range(4):
                put("pe", lambda e, kt=kt: three(e, bank[:, :], ahi[:, kt, :], alo[:, kt, :], WL["o", "h"][:, kt, :], WL["o", "l"][:, kt, :], kt == 0),
                    None, [("ahi", g), ("alo", g), *mw_done[b, 1], *free])
            put("pe", lambda e: mm(e, bank[:, :], selT[:, 1, :], biasT[:, :]), ("O", g), [])
            put("dve", lambda e: e.tensor_tensor(xs[:, :], bank[:, :], xs[:, :], ALU.add), ("x1", g), [("O", g), (f"ldt{g % 4}", g)])
            tok_free[s] = (("x1", g),)
            put("dve", lambda e: e.bn_stats(st1, xs[:, :]), ("b1", g), [("x1", g)])
            put("dve", lambda e: e.bn_aggr(mv1, st1), ("a1", g), [("b1", g), ("z", g - 1)])
            put("pool", lambda e: e.tensor_tensor(rs1[:, 0:1], mv1[:, 1:2], eps5, ALU.add), ("r1a", g), [("a1", g), ("c_eps", 0), ("r1", g - 1)])
            put("pool", lambda e: e.tensor_tensor(rs1[:, 1:2], rs1[:, 0:1], mh, ALU.pow), ("r1", g), [("r1a", g), ("z", g - 1), ("c_cst", 0)])
            put("dve", lambda e: e.tensor_scalar(z[:, :], xs[:, :], mv1[:, 0:1], rs1[:, 1:2], ALU.subtract, ALU.mult), ("z", g), [("r1", g), ("zTr", g - 1), ("v1", g - 1)])

        def stage_v(g):
            pg, pb = pgb[:, 0:512], pgb[:, 512:1024]
            put("pool", lambda e: e.tensor_tensor(pg, z[:, :], pg, ALU.mult), ("v1", g), [("z", g), ("gat", g)])
            put("pool", lambda e: e.tensor_tensor(pg, pg, pb, ALU.add), ("v2", g), [("v1", g)])
            put("dve", lambda e: e.bn_stats(st2_, pg), ("b2", g), [("v2", g)])
            put("dve", lambda e: e.bn_aggr(mv2, st2_), ("a2", g), [("b2", g), ("u", g - 1)])
            put("pool", lambda e: e.tensor_tensor(rs2[:, 0:1], mv2[:, 1:2], eps5, ALU.add), ("r2a", g), [("a2", g), ("r2", g - 1)])
            put("pool", lambda e: e.tensor_tensor(rs2[:, 1:2], rs2[:, 0:1], mh, ALU.pow), ("r2", g), [("r2a", g), ("u", g - 1)])
            put("dve", lambda e: e.tensor_scalar(pg, pg, mv2[:, 0:1], rs2[:, 1:2], ALU.subtract, ALU.mult), ("u", g), [("r2", g), ("v2", g)])

        def gather(g):
            off = bass.IndirectOffsetOnAxis(ap=pidx[:, g:g + 1].bitcast(U32), axis=0)
            put("pool", lambda e: e.indirect_dma_start(pgb[:, :], None, A["pw"], off), ("gat", g), [("uTr", g - 1), ("v2", g - 1), ("c_pidx", 0)], dma=True)

        def xpose(g, src, needs, key):
            s, bank, free = xp_bank()
            for c in range(4):
                put("pe", lambda e, c=c: e.transpose(bank[:, c * 128:c * 128 + 128], src[:, c * 128:c * 128 + 128], ident[:, :]),
                    key if c == 3 else None, [*needs, ("c_id", 0), *free])
            return s, bank[:, :].rearrange("p (c t) -> p c t", c=4)

        def half(g):
            return slice((g % 2) * 128, (g % 2) * 128 + 128)

        def stage_x1T(g):
            k = g // 2
            s, v = xpose(g, xb[g % 4], [("x1", g)], ("xTr", g))
            h = half(g)
            put("act", lambda e: e.copy(op[0]["h"][:, :, h], v), ("oxh", g), [("xTr", g), ("W2", 2 * k - 1), *pro_end])
            put("dve", lambda e: e.tensor_tensor(op[0]["l"][:, :, h], v, op[0]["h"][:, :, h].bitcast(F32), ALU.subtract), ("oxl", g), [("oxh", g), ("W2", 2 * k - 1)])
            xp_free[s] = (("oxl", g),)
            put("pool", lambda e: e.tensor_tensor(xb[g % 4][:, :], xb[g % 4][:, :], beint[:, :], ALU.add), ("xbe", g), [("xTr", g), ("z", g), ("b1", g), ("c_be", 0)])

        def stage_zT(g):
            s, v = xpose(g, z, [("z", g)], ("zTr", g))
            put("act", lambda e: e.copy(zT[:, :, half(g)], v), ("zT", g), [("zTr", g), ("prod_s", g - 2), ("prod_t", g - 2), *pro_end])
            xp_free[s] = (("zT", g),)

        def stage_uT(g):
            s, v = xpose(g, pgb, [("u", g)], ("uTr", g))
            put("act", lambda e: e.copy(uT[:, :, :], v), ("uT", g), [("uTr", g), ("prod_h", g - 1), *pro_end])
            xp_free[s] = (("uT", g),)

        def one_hot(k):
            s = k % 2
            used = [("W1x1", k - 2), ("Gs", 2 * k - 3), ("Gh", 2 * k - 3)]
            rd = [("oh", k - 1)]
            t = slice(k * 256, k * 256 + 256)
            for i, nm in enumerate(("cid", "sid", "bid")):
                put("sp", lambda e, i=i, nm=nm: e.dma_start(ids[32 * i:32 * i + 32, :], A[nm][t].partition_broadcast(32)),
                    ("ids", k * 3 + i), [*rd, ("c_ids", 0)], dma=True)
            put("dve", lambda e: e.tensor_scalar(OH[s][:, :], ids[:, :], cst[:, 0:1], None, ALU.is_equal), ("oh", k), [("ids", k * 3 + 2), ("c_cst", 0), *used])

        def product(g, name, src, srckey, slot, freekeys):
            k = g // 2
            s, bank, free = xp_bank()
            tab = GT[name]
            nG = {"t": 0, "s": 1, "h": 2}[name]
            for c in range(4):
                put("pe", lambda e, c=c: mm(e, bank[:, c * 128:c * 128 + 128], tab[:, c * 128:c * 128 + 128], OH[k % 2][:, half(g)], start=(c == 0)),
                    ("G" + name, g) if c == 3 else None, [("oh", k), ("s3_6", 1 + nG), *free])
            ys, y, yf = y_buf()
            yv = y[:, :].rearrange("p (c t) -> p c t", c=4)
            put("dve", lambda e: e.tensor_tensor(yv, src, bank[:, :].rearrange("p (c t) -> p c t", c=4), ALU.mult), ("prod_" + name, g), [("G" + name, g), srckey, *yf])
            xp_free[s] = (("prod_" + name, g),)
            h = half(g)
            put("act", lambda e: e.copy(op[slot]["h"][:, :, h], yv), (f"o{name}h", g), [("prod_" + name, g), *freekeys])
            put("pool", lambda e: e.tensor_tensor(op[slot]["l"][:, :, h], yv, op[slot]["h"][:, :, h].bitcast(F32), ALU.subtract), (f"o{name}l", g), [(f"o{name}h", g), *freekeys])
            y_free[ys] = ((f"o{name}l", g),)

        def stage_t(g):
            product(g, "t", zT[:, :, half(g)], ("zT", g), 1, [("W1h1", g // 2 - 1)])

        def stage_s(g):
            product(g, "s", zT[:, :, half(g)], ("zT", g), 0, [("W1x1", g // 2)])

        def stage_h(g):
            product(g, "h", uT[:, :, :], ("uT", g), 1, [("W1t1", g // 2)])

        slot_of = {"x": 0, "t": 1, "s": 0, "h": 1}

        def stage_W1(k, name, pair):
            acc = ps[f"acc{pair}"]
            o = op[slot_of[name]]
            needs = [(f"o{name}h", 2 * k + 1), (f"o{name}l", 2 * k + 1), *w1_done[name]]
            for j in range(2):
                m = 2 * pair + j
                dst = acc[:, j * 256:j * 256 + 256]
                ms = slice(m * 128, m * 128 + 128)
                if name == "x":
                    put("pe", lambda e, j=j, dst=dst, ms=ms: mm(e, dst, PT[:, ms], OH[k % 2][:, :], start=(j == 0)), None,
                        [("sil", 2 * (k - 1) + pair), ("oh", k), ("s3_6", 4)])
                for kt in range(4):
                    put("pe", lambda e, kt=kt, dst=dst, ms=ms: three(e, dst, W1[name, "h"][:, kt, ms], W1[name, "l"][:, kt, ms], o["h"][:, kt, :], o["l"][:, kt, :], False),
                        (f"W1{name}{pair}", k) if (j == 1 and kt == 3) else None, needs)

        def stage_silu(k, pair):
            ys, y, yf = y_buf()
            n = 2 * k + pair
            acc = ps[f"acc{pair}"]
            c = slice(2 * pair, 2 * pair + 2)
            put("act", lambda e: e.activation(y[:, :], acc[:, :], ACT.Silu), ("sil", n), [(f"W1h{pair}", k), *yf])
            hv = lambda p: op[0][p][:, c, :].rearrange("p a b -> p (a b)")
            put("act", lambda e: e.copy(hv("h"), y[:, :]), ("ash", n), [("sil", n), ("W1s1", k)])
            put("dve", lambda e: e.tensor_tensor(hv("l"), y[:, :], hv("h").bitcast(F32), ALU.subtract), ("asl", n), [("ash", n), ("W1s1", k)])
            y_free[ys] = (("asl", n),)

        def stage_W2(g):
            k = g // 2
            s, bank, free = tok_bank()
            for m in range(4):
                put("pe", lambda e, m=m: three(e, bank[:, :], op[0]["h"][:, m, half(g)], op[0]["l"][:, m, half(g)], WL["2", "h"][:, m, :], WL["2", "l"][:, m, :], m == 0),
                    None, [("ash", 2 * k + 1), ("asl", 2 * k + 1), *w2_done[0], *free])
            put("pe", lambda e: mm(e, bank[:, :], selT[:, 2, :], biasT[:, :]), ("W2", g), [])
            xs = xb[g % 4]
            put("dve", lambda e: e.bn_stats(st3, bank[:, :]), ("b3", g), [("W2", g)])
            put("dve", lambda e: e.bn_aggr(mv3, st3), ("a3", g), [("b3", g), ("w", g - 1)])
            put("pool", lambda e: e.tensor_tensor(rs3[:, 0:1], mv3[:, 1:2], eps5, ALU.add), ("r3a", g), [("a3", g), ("r3", g - 1)])
            put("pool", lambda e: e.tensor_tensor(rs3[:, 1:2], rs3[:, 0:1], mh, ALU.pow), ("r3", g), [("r3a", g), ("fin", g - 1)])
            ys, y, yf = y_buf()
            put("dve", lambda e: e.scalar_tensor_tensor(out=y[:, :], in0=bank[:, :], scalar=mv3[:, 0:1], in1=gint[:, :], op0=ALU.subtract, op1=ALU.mult),
                ("w", g), [("a3", g), ("c_gi", 0), *yf])
            tok_free[s] = (("w", g),)
            put("dve", lambda e: e.scalar_tensor_tensor(out=xs[:, :], in0=y[:, :], scalar=rs3[:, 1:2], in1=xs[:, :], op0=ALU.mult, op1=ALU.add),
                ("fin", g), [("w", g), ("r3", g), ("xbe", g)])
            y_free[ys] = (("fin", g),)
            put("sp", lambda e: e.dma_start(out[g * 128:g * 128 + 128, :], xs[:, :]), (f"out{g % 4}", g), [("fin", g)], dma=True)

        pro_end = []

        consts()
        styles()
        put("dve", lambda e: e.memset(P["tabT"][:, :, :], 0.0), ("tz", 0))
        bias_table()
        load_x(0)
        split_x(0)
        mod_weights(0, 0)
        load_x(1)
        for g in range(2):
            load_tok(g)
        stage_A(0)
        stage_bdq(0)
        stage_V(0)
        split_x(1)
        weights_softmax()

        for k in range(NT + 1):
            a, b = 2 * k, 2 * k + 1
            front, back = k < NT, k > 0
            if front:
                stage_S(a)
                stage_A(b)
                if b + 1 < NG:
                    load_x(b + 1)
                if a % 8 == 0:
                    mod_weights(a // 8, 1)
            if back:
                stage_W1(k - 1, "x", 0)
                stage_W1(k - 1, "x", 1)
                stage_s(a - 2)
                stage_s(a - 1)
                stage_W1(k - 1, "t", 0)
            else:
                g_tables()
                mlp()
                table_T()
            if front:
                stage_AV(a)
            if back:
                stage_W1(k - 1, "t", 1)
                stage_h(a - 2)
                stage_uT(a - 1)
                stage_h(a - 1)
            if front:
                gather(a)
                stage_aTr(a)
                stage_bdq(b)
                stage_V(b)
                if k == 0:
                    w1_and_P()
                    w2_weights()
                    pro_end.extend([("Pm", 23), ("s3_6", 4), ("mh2", 0), ("wl", nw[0] - 1), ("wh", nw[0] - 1), ("pbs", 0)])
                stage_S(b)
                stage_O(a)
            if back:
                stage_W1(k - 1, "s", 0)
                stage_W1(k - 1, "s", 1)
            if front:
                stage_v(a)
                stage_AV(b)
            if back:
                stage_W1(k - 1, "h", 0)
                stage_silu(k - 1, 0)
                stage_W1(k - 1, "h", 1)
                stage_silu(k - 1, 1)
            if front:
                stage_aTr(b)
                one_hot(k)
                if b + 1 < NG:
                    split_x(b + 1)
                    if (b + 1) % 8 == 0:
                        mod_weights((b + 1) // 8, 0)
                    stage_A(b + 1)
                    load_x(b + 2)
                    split_x(b + 2)
                stage_zT(a)
                stage_O(b)
                stage_t(a)
                stage_uT(a)
                gather(b)
            if back:
                stage_W2(a - 2)
                stage_W2(a - 1)
            if front:
                if b + 1 < NG:
                    load_tok(b + 1)
                    load_tok(b + 2)
                stage_x1T(a)
                stage_zT(b)
                stage_t(b)
                stage_x1T(b)
                stage_v(b)
                if b + 1 < NG:
                    stage_bdq(b + 1)
                    stage_V(b + 1)
        for s in range(4):
            put("sp", None, None, [(f"out{s}", NG - 4 + s)])

        sems = {n: ctx.enter_context(nc.semaphore("s_" + n)) for n in Q.count}
        block = ctx.enter_context(nc.Block())

        @block.sync
        def _(e):
            Q.emit("sp", e, sems)

        @block.tensor
        def _(e):
            Q.emit("pe", e, sems)

        @block.scalar
        def _(e):
            Q.emit("act", e, sems)

        @block.vector
        def _(e):
            Q.emit("dve", e, sems)

        @block.gpsimd
        def _(e):
            Q.emit("pool", e, sems)


NAMES = ["cond_512", "cond_64", "fside_Bx32_0"]


def kernel(**inp):
    import ml_dtypes
    import concourse.bacc as bacc
    from concourse.bass_utils import run_bass_kernel_spmd

    bf = ml_dtypes.bfloat16
    get = lambda n: np.asarray(inp[n])
    c = lambda x: np.ascontiguousarray(x)
    L0 = lambda n: get("L0_cond_" + n)
    L1 = lambda n: get("L1_cond_" + n)
    x = get("x").reshape(4096, 512)
    arr = {"x": c(x), "xT": c(x.reshape(NG, 128, 4, 128).transpose(0, 3, 2, 1))}

    def blocks(w, rows=None):
        n = w.shape[0]
        m = -(-n // 128)
        o = np.zeros((m * 128, w.shape[1]), w.dtype)
        o[:n] = w
        return c(o.reshape(m, 128, w.shape[1]))

    for s in "ko":
        arr[s + "_affT"] = blocks(L0(s + "_aff_w").T)
        arr[s + "_wT"] = blocks(L0(s + "_w").T)
    arr["affb"] = c(np.stack([L0("k_aff_b").reshape(4, 128).T, L0("o_aff_b").reshape(4, 128).T], 1))
    cond = np.zeros((4, 128, 4), np.float32)
    cond[0:2] = get("cond_512").T.reshape(2, 128, 4)
    cond[2, 0:64] = get("cond_64").T
    cond[3, 0:32] = get("fside_Bx32_0").T
    arr["condT"] = c(cond.transpose(1, 0, 2))
    arr["kb"], arr["ob"] = c(L0("k_b").reshape(1, 512)), c(L0("o_b").reshape(1, 512))
    arr["b2"] = c(L1("int_b2").reshape(1, 512))
    arr["pw"] = c(np.concatenate([L1("pw_g"), L1("pw_b")], 1))
    for n in ("cp_g", "tm_g", "ms_g", "cp_b", "tm_b", "ms_b", "int_b1", "int_g", "int_be", "aw"):
        arr[n] = c(L1(n))
    for n in ("mem", "noi", "res"):
        arr[n + "_w1"] = blocks(L1(n + "_W1"))
        arr[n + "_w2"] = blocks(L1(n + "_W2"))
        for t in ("_b1", "_b2", "_g", "_be"):
            arr[n + t] = c(L1(n + t))
    arr["int_w1"] = blocks(L1("int_W1"))
    arr["int_w2"] = blocks(L1("int_W2"))
    arr["cid"] = c(get("itok_BxS_0_4").reshape(-1))
    arr["sid"] = c(get("mask_BxS_ik0").reshape(-1))
    arr["pidx"] = c(get("itok_BxS_0_999").reshape(NG, 128).T)
    arr["bid"] = np.repeat(np.arange(4, dtype=np.int32), 1024)
    p = np.arange(128)
    cst = np.zeros((128, 5), np.float32)
    n_of = {0: 5, 1: 3, 2: 4, 3: 0}
    cst[:, 0] = [(i % 8) if (i % 32) < 24 and (i % 8) < n_of[i // 32] else -1 for i in p]
    for j in range(3):
        cst[:, 1 + j] = (p % 32) // 8 == j
    cst[:, 4] = -0.5
    arr["cst"] = cst
    arr["ident"] = np.eye(128, dtype=np.float32)
    arr["selT"] = c(np.broadcast_to((p[:, None] // 32 == np.arange(3)[None])[:, :, None], (128, 3, 128)).astype(bf))
    t2 = (p % 32) // 16
    arr["maskL"] = (np.where(p[:, None] == t2[None], np.float32(NEG), np.float32(0))).astype(bf)
    m = np.arange(32) // 16
    arr["maskR"] = ((p[:, None] != m[None]) & (p[:, None] < 2)).astype(bf)

    nc = bacc.Bacc("TRN2", target_bir_lowering=False, num_devices=1)
    A = {n: nc.dram_tensor("in_" + n, a.shape, mybir.dt.from_np(a.dtype), kind="ExternalInput").ap() for n, a in arr.items()}
    out = nc.dram_tensor("out", (4096, 512), F32, kind="ExternalOutput").ap()
    build(nc, A, out)
    r = run_bass_kernel_spmd(nc, [{"in_" + n: a for n, a in arr.items()}], core_ids=[0])
    return r.results[0]["out"].reshape(4, 1024, 512)
```

```python
import numpy as np
import concourse.bass as bass
from concourse import mybir
from contextlib import ExitStack

F32 = mybir.dt.float32
F32R = mybir.dt.float32r
BF16 = mybir.dt.bfloat16
F16 = mybir.dt.float16
I32 = mybir.dt.int32
U32 = mybir.dt.uint32
ALU = mybir.AluOpType
ACT = mybir.ActivationFunctionType
AX = mybir.AxisListType

NG = 32
NT = 16
SCALE = 32.0 ** -0.5
NEG = -1.0e30

PROLOGUE = set("""c_eps c_z c_bd12 c_bd3 c_ids sty styl stsq wsq dmm dme dmp s3_0 s3_1 s3_2 s3_3 s3_4 s3_5
s3_6 wm ws we wd wr w6 gw mz m1 mh mh2 mt mhT m2 mv0 mv1 mv2 mv3 mv4 mv5 mv6 mv7 mu vT lz lb Pm xa wh wl
pbs""".split())


class Queues:

    def __init__(self):
        self.items = {e: [] for e in ("pe", "act", "dve", "pool", "sp")}
        self.count = {}
        self.value = {}
        self.owner = {}

    def put(self, eng, fn, key=None, needs=(), dma=False):
        waits = []
        for n in needs:
            if n is not None and n[1] >= 0:
                waits.append(self.value[n])
        inc = None
        if key is not None:
            step = 16 if dma else 1
            name = "pro_" + eng if key[0] in PROLOGUE else key[0]
            assert self.owner.setdefault(name, eng) == eng, key
            self.count[name] = self.count.get(name, 0) + step
            self.value[key] = (name, self.count[name])
            inc = (name, step)
        self.items[eng].append((waits, fn, inc))

    def emit(self, eng, e, sems):
        seen = {}
        for waits, fn, inc in self.items[eng]:
            for stage, v in waits:
                if seen.get(stage, 0) < v:
                    e.wait_ge(sems[stage], v)
                    seen[stage] = v
            if fn is None:
                continue
            i = fn(e)
            if inc:
                i.then_inc(sems[inc[0]], inc[1])


def build(nc, A, out):
    Q = Queues()
    put = Q.put
    ctx = ExitStack()
    with ctx:
        def sb(name, shape, dt=F32, c=ctx):
            return c.enter_context(nc.sbuf_tensor(name, shape, dt))

        ident = sb("ident", [128, 128])
        cst = sb("cst", [128, 5])
        selT = sb("selT", [128, 3, 128], BF16)
        maskL = sb("maskL", [128, 128], BF16)
        maskR = sb("maskR", [128, 32], BF16)
        gint = sb("gint", [128, 512])
        beint = sb("beint", [128, 512])
        biasT = sb("biasT", [128, 512], BF16)
        GT = {n: sb("G" + n, [128, 512], BF16) for n in "ths"}
        PT = sb("PT", [128, 512], BF16)
        w6 = sb("w6", [128, 6])
        styl = sb("styl", [128, 2, 4, 4])
        dmT = sb("dmT", [128, 2, 16])
        pidx = sb("pidx", [128, NG], I32)
        W1 = {(n, p): sb(f"W1{n}{p}", [128, 4, 512], F32R) for n in "xtsh" for p in "hl"}
        WL = {(n, p): sb(f"W{n}{p}", [128, 4, 512], F32R) for n in ("k", "o", "2") for p in "hl"}
        NRING = 2
        ring = [sb(f"ring{i}", [128, 512])[:, :] for i in range(NRING)]
        ytmp = [sb(f"ytmp{i}", [128, 512]) for i in range(2)]
        small = sb("small", [128, 96])
        eps5 = small[:, 0:1]
        mh = cst[:, 4:5]

        ids = sb("ids", [128, 256], I32)
        OH = [sb(f"OH{i}", [128, 256], BF16) for i in range(2)]
        xraw = sb("xraw", [128, 4, 128])
        xhi = sb("xhi", [128, 4, 128], F32R)
        xlo = sb("xlo", [128, 4, 128], F32R)
        q = sb("q", [128, 512])
        q12 = sb("q12", [128, 512, 2], BF16)
        q3 = sb("q3", [128, 512], BF16)
        v12 = sb("v12", [128, 512, 2], BF16)
        v3 = sb("v3", [128, 512], BF16)
        BD12 = sb("BD12", [128, 16, 4, 32, 2], BF16)
        BD3 = sb("BD3", [128, 16, 4, 32], BF16)
        SE = sb("SE", [128, 512])
        ET = sb("ET", [128, 512])
        e12 = sb("e12", [128, 512, 2], F16)
        ahi = sb("ahi", [128, 4, 128], F32R)
        alo = sb("alo", [128, 4, 128], F32R)
        xb = [sb(f"xb{i}", [128, 512]) for i in range(4)]
        ps = {n: ctx.enter_context(nc.psum_tensor(n, [128, 512], F32))
              for n in ("acc0", "acc1", "tok0", "tok1", "att0", "att1", "xp0", "xp1")}
        main = ExitStack()
        pro = ExitStack()
        with pro:
            psb = lambda n, s, d=F32: sb(n, s, d, pro)
            P = dict(
                h=psb("p_h", [128, 512]), hT=psb("p_hT", [128, 4, 128]),
                L0=psb("p_L0", [128, 4, 96]), L1=psb("p_L1", [128, 4, 96]), L2=psb("p_L2", [128, 4, 96]),
                t0=psb("p_t0", [128, 512]), t1=psb("p_t1", [128, 512]), t2=psb("p_t2", [128, 512]),
                tabT=psb("p_tabT", [128, 4, 128]),
                condT=psb("p_condT", [128, 4, 4]), abc=psb("p_abc", [128, 2, 4]),
                aw=psb("p_aw", [128, 6]), st2=psb("p_st2", [128, 2, 4, 4]), v=psb("p_v", [128, 2, 16]),
                r0=psb("p_r0", [128, 512]), r1=psb("p_r1", [128, 512]),
            )
        ctx.enter_context(main)
        msb = lambda n, s, d=F32: sb(n, s, d, main)
        op = [{p: msb(f"op{i}{p}", [128, 4, 256], F32R) for p in "hl"} for i in range(2)]
        zT = msb("zT", [128, 4, 256])
        uT = msb("uT", [128, 4, 128])
        z = sb("z", [128, 512])
        pgb = sb("pgb", [128, 1024])
        dmb = sb("dmb", [128, 512])

        tok_n = [0]
        tok_free = [(), ()]
        xp_n = [0]
        xp_free = [(), ()]

        def tok_bank():
            s = tok_n[0] % 2
            tok_n[0] += 1
            free, tok_free[s] = tok_free[s], None
            return s, ps[f"tok{s}"], free

        def xp_bank():
            s = xp_n[0] % 2
            xp_n[0] += 1
            free, xp_free[s] = xp_free[s], None
            return s, ps[f"xp{s}"], free

        y_n = [0]
        y_free = [(), ()]

        def y_buf():
            s = y_n[0] % 2
            y_n[0] += 1
            free, y_free[s] = y_free[s], None
            return s, ytmp[s], free

        slots = [(f"ring{i}", t) for i, t in enumerate(ring)]
        r_n = [0]
        r_free = {}
        r_use = {}

        def load_chunk(src, slot=None):
            if slot is None:
                slot = slots[r_n[0] % len(slots)]
                r_n[0] += 1
            name, t = slot
            n = r_use[name] = r_use.get(name, -1) + 1
            free, r_free[name] = r_free.get(name, ()), None
            put("sp", lambda e: e.dma_start(t, src), (name, n), free, dma=True)
            return name, t, (name, n)

        def mm(e, o, a, b, start=False):
            return e.matmul(o, a, b, start=start, stop=True, skip_group_check=True)

        def three(e, o, ah, al, bh, bl, start):
            mm(e, o, ah, bh, start)
            mm(e, o, ah, bl)
            return mm(e, o, al, bh)

        def consts():
            put("sp", lambda e: e.dma_start(P["condT"][:, :, :], A["condT"]), ("c_cond", 0), dma=True)
            put("act", lambda e: e.dma_start(P["abc"][:, :, :], A["affb"]), ("c_abc", 0), dma=True)
            put("act", lambda e: e.dma_start(cst[:, :], A["cst"]), ("c_cst", 0), dma=True)
            put("act", lambda e: e.dma_start(ident[:, :], A["ident"]), ("c_id", 0), dma=True)
            put("act", lambda e: e.dma_start(P["t0"][:, :], A["rows_b"]), ("c_rb", 0), dma=True)
            put("act", lambda e: e.dma_start(selT[:, :, :], A["selT"]), ("c_sel", 0), dma=True)
            put("dve", lambda e: e.memset(eps5, 1e-5), ("c_eps", 0))
            put("dve", lambda e: e.memset(P["L2"][:, :, :], 0.0), ("c_z", 0))
            put("pool", lambda e: e.memset(BD12[:, :, :, :, :].bitcast(U32), 0), ("c_bd12", 0))
            put("pool", lambda e: e.memset(BD3[:, :, :, :].bitcast(U32), 0), ("c_bd3", 0))
            put("pool", lambda e: e.memset(ids[:, :], 0), ("c_ids", 0))

        def consts2():
            put("act", lambda e: e.dma_start(maskL[:, :], A["maskL"]), ("c_mL", 0), dma=True)
            put("act", lambda e: e.dma_start(maskR[:, :], A["maskR"]), ("c_mR", 0), dma=True)
            put("act", lambda e: e.dma_start(P["aw"][:, :], A["aw"].partition_broadcast(128)), ("c_aw", 0), dma=True)
            put("act", lambda e: e.dma_start(pidx[:, :], A["pidx"]), ("c_pidx", 0), dma=True)
            put("act", lambda e: e.dma_start(P["tabT"][:, :, :], A["tabT"]), ("c_tabT", 0), dma=True)
            put("act", lambda e: e.dma_start(gint[:, :], A["int_g"].partition_broadcast(128)), ("c_gi", 0), dma=True)
            put("act", lambda e: e.dma_start(beint[:, :], A["int_be"].partition_broadcast(128)), ("c_be", 0), dma=True)

        def split3(src, dst, tag, needs):
            a, b = P["t1"], P["t2"]
            p1, p2 = b[:, 0:256].bitcast(BF16), b[:, 256:512].bitcast(BF16)
            k = lambda i: (f"s3_{i}", tag)
            put("dve", lambda e: e.tensor_copy(p1, src), k(0), list(needs) + [("s3_5", tag - 1)])
            put("dve", lambda e: e.tensor_tensor(src, src, p1, ALU.subtract), k(1), [k(0)])
            put("dve", lambda e: e.tensor_scalar(a[:, :], p1, cst[:, 1:2], None, ALU.mult), k(2), [k(0), ("c_cst", 0), ("s3_6", tag - 1)])
            put("dve", lambda e: e.tensor_copy(p2, src), k(3), [k(1)])
            put("dve", lambda e: e.tensor_tensor(src, src, p2, ALU.subtract), k(4), [k(3)])
            put("dve", lambda e: e.scalar_tensor_tensor(out=a[:, :], in0=p2, scalar=cst[:, 2:3], in1=a[:, :], op0=ALU.mult, op1=ALU.add), k(5), [k(2), k(3)])
            put("dve", lambda e: e.scalar_tensor_tensor(out=dst, in0=src, scalar=cst[:, 3:4], in1=a[:, :], op0=ALU.mult, op1=ALU.add), k(6), [k(4), k(5)])

        def bias_table():
            split3(P["t0"][:, :], biasT[:, :], 0, [("c_rb", 0)])

        def g_table(n):
            name, w = (("t", 1), ("s", 5), ("h", 0))[n]
            put("sp", lambda e: e.dma_start(P["t0"][:, :], A["rows_" + name]), ("gl", n), [("s3_6", n)], dma=True)
            put("dve", lambda e: e.tensor_scalar(P["t0"][:, :], P["t0"][:, :], w6[:, w:w + 1], None, ALU.mult),
                ("gw", n), [("gl", n), ("w6", 0)])
            split3(P["t0"][:, :], GT[name][:, :], 1 + n, [("gw", n)])

        def weights_softmax():
            aw = P["aw"]
            put("dve", lambda e: e.tensor_reduce(small[:, 1:2], aw[:, :], axis=AX.X, op=ALU.max), ("wm", 0), [("c_aw", 0)])
            put("dve", lambda e: e.tensor_scalar(aw[:, :], aw[:, :], small[:, 1:2], None, ALU.subtract), ("ws", 0), [("wm", 0)])
            put("act", lambda e: e.activation(aw[:, :], aw[:, :], ACT.Exp), ("we", 0), [("ws", 0)])
            put("dve", lambda e: e.tensor_reduce(small[:, 2:3], aw[:, :], axis=AX.X, op=ALU.add), ("wd", 0), [("we", 0)])
            put("dve", lambda e: e.reciprocal(small[:, 3:4], small[:, 2:3]), ("wr", 0), [("wd", 0)])
            put("dve", lambda e: e.tensor_scalar(w6[:, :], aw[:, :], small[:, 3:4], None, ALU.mult), ("w6", 0), [("wr", 0)])

        aff_slots = ((None, None), (("cSE", SE[:, :]), ("cET", ET[:, :])))
        w_slots = ((("cr0", P["r0"][:, :]), ("cr1", P["r1"][:, :]), ("cxb2", xb[2][:, :]), ("cxb3", xb[3][:, :])),
                   (("pgb0", pgb[:, 0:512]), ("pgb1", pgb[:, 512:1024]), ("cz", z[:, :]), ("ph", P["h"][:, :])))

        def style(L):
            nm = "ko"[L]
            s, bank, free = xp_bank()
            cs = [load_chunk(A[nm + "_affT"][st], aff_slots[L][st]) for st in range(2)]
            for kt in range(4):
                for st in range(2):
                    put("pe", lambda e, kt=kt, st=st: mm(
                        e, bank[:, kt * 4:kt * 4 + 4], cs[st][1][:, kt * 128:kt * 128 + 128], P["condT"][:, st, :], start=(kt == 0 and st == 0)),
                        ("sty", L) if (kt == 3 and st == 1) else None, [cs[st][2], ("c_cond", 0), *free])
            for c in cs:
                r_free[c[0]] = (("sty", L),)
            put("dve", lambda e: e.tensor_tensor(
                styl[:, L, :, :], bank[:, 0:16].rearrange("p (k b) -> p k b", b=4),
                P["abc"][:, L, :].unsqueeze(2).to_broadcast([128, 4, 4]), ALU.add), ("styl", L), [("sty", L), ("c_abc", 0)])
            xp_free[s] = (("styl", L),)
            put("dve", lambda e: e.tensor_tensor(P["st2"][:, L, :, :], styl[:, L, :, :], styl[:, L, :, :], ALU.mult), ("stsq", L), [("styl", L)])

        def demodulation(L):
            nm = "ko"[L]
            cs = kept[L] = [load_chunk(A[nm + "_wT"][kt], w_slots[L][kt]) for kt in range(4)]
            s, bank, free = xp_bank()
            for kt in range(4):
                c = cs[kt]
                ys, y, yf = y_buf()
                put("act", lambda e, c=c, y=y: e.activation(y[:, :], c[1], ACT.Square), ("wsq", L * 4 + kt), [c[2], *yf])
                for ob in range(4):
                    put("pe", lambda e, y=y, kt=kt, ob=ob: mm(e, bank[:, ob * 4:ob * 4 + 4], y[:, ob * 128:ob * 128 + 128], P["st2"][:, L, kt, :], start=(kt == 0 and ob == 0)),
                        ("dmm", L * 4 + kt) if ob == 3 else None, [("wsq", L * 4 + kt), ("stsq", L), *free])
                y_free[ys] = (("dmm", L * 4 + kt),)
            v = P["v"][:, L, :]
            put("dve", lambda e: e.tensor_scalar(v, bank[:, 0:16], 1e-8, None, ALU.add), ("dme", L), [("dmm", L * 4 + 3)])
            xp_free[s] = (("dme", L),)
            put("pool", lambda e: e.tensor_tensor(dmT[:, L, :], v, mh.to_broadcast([128, 16]), ALU.pow), ("dmp", L), [("dme", L), ("c_cst", 0)])

        kept = {}

        def mod_weights(b, L):
            nm = "ko"[L]
            n = b * 2 + L
            last_use = ("A", 8 * b - 1) if L == 0 else ("O", 8 * b - 1)
            s, bank, free = xp_bank()
            for ob in range(4):
                put("pe", lambda e, ob=ob: mm(e, bank[:, ob * 128:ob * 128 + 128], dmT[:, L, ob * 4 + b:ob * 4 + b + 1].to_broadcast([128, 128]), ident[:, :], start=(ob == 0)),
                    ("dbc", n) if ob == 3 else None, [("dmp", L), ("c_id", 0), *free])
            put("act", lambda e: e.copy(dmb[:, :], bank[:, :]), ("dmb", n), [("dbc", n), ("stt", 4 * n - 1)])
            xp_free[s] = (("dmb", n),)
            for kt in range(4):
                c = kept[L][kt] if b == 0 else load_chunk(A[nm + "_wT"][kt])
                ys, y, yf = y_buf()
                i = 4 * n + kt
                put("dve", lambda e, c=c, y=y, kt=kt: e.scalar_tensor_tensor(
                    out=y[:, :], in0=c[1], scalar=styl[:, L, kt, b:b + 1], in1=dmb[:, :], op0=ALU.mult, op1=ALU.mult),
                    ("stt", i), [c[2], ("dmb", n), ("styl", L), *yf])
                r_free[c[0]] = (("stt", i),)
                put("act", lambda e, y=y, kt=kt: e.copy(WL[nm, "h"][:, kt, :], y[:, :]), ("mwh", i), [("stt", i), last_use])
                put("dve", lambda e, y=y, kt=kt: e.tensor_tensor(WL[nm, "l"][:, kt, :], y[:, :], WL[nm, "h"][:, kt, :].bitcast(F32), ALU.subtract),
                    ("mwl", i), [("mwh", i), last_use])
                y_free[ys] = (("mwl", i),)
            mw_done[b, L] = [("mwh", 4 * n + 3), ("mwl", 4 * n + 3)]

        mw_done = {}
        nw = [0]

        def split_weight(y, ykeys, H, Lo, kt, eng):
            i = nw[0]
            nw[0] += 1
            put("act", lambda e: e.copy(H[:, kt, :], y), ("wh", i), ykeys)
            put(eng, lambda e: e.tensor_tensor(Lo[:, kt, :], y, H[:, kt, :].bitcast(F32), ALU.subtract), ("wl", i), [("wh", i)])
            return (("wh", i), ("wl", i))

        def w2_weights():
            for kt in range(4):
                cs, c, key = load_chunk(A["int_w2"][kt])
                rd = split_weight(c, [key], WL["2", "h"], WL["2", "l"], kt, ("dve", "pool")[kt % 2])
                r_free[cs] = rd
                w2_done[0] = [*w2_done[0], *rd]

        w2_done = [()]

        nets = [("mem", 0, (0, 1)), ("noi", 32, (2,)), ("res", 64, (3,))]

        def zeros(bank, i, needs):
            z0 = P["L2"][:, :, :].rearrange("p a b -> p (a b)")
            put("pe", lambda e: mm(e, bank[:, 0:384], z0[:, 0:128], z0, start=True), None, needs)
            put("pe", lambda e: mm(e, bank[:, 384:512], z0[:, 0:128], z0[:, 0:128]), ("mz", i))

        def mlp1():
            h, hT = P["h"], P["hT"]
            bank = ps["acc1"]
            zeros(bank, 0, [("c_z", 0)])
            for i, (n, r, cs_) in enumerate(nets):
                for j, ci in enumerate(cs_):
                    sl, c, key = load_chunk(A[n + "_w1"][j])
                    put("pe", lambda e, r=r, ci=ci, c=c: mm(e, bank[r:r + 4, :], P["condT"][:, ci, :], c), ("m1", i * 2 + j), [key])
                    r_free[sl] = (("m1", i * 2 + j),)
            cv = load_chunk(A["rows_v"][0])
            put("dve", lambda e: e.tensor_tensor(h[:, :], bank[:, :], cv[1], ALU.add), ("mh", 0), [("m1", 4), cv[2], ("stt", 7)])
            r_free[cv[0]] = (("mh", 0),)
            put("act", lambda e: e.activation(h[:, :], h[:, :], ACT.Silu), ("mh2", 0), [("mh", 0)])
            s, bank2, free = xp_bank()
            for kt in range(4):
                put("pe", lambda e, kt=kt: e.transpose(bank2[:, kt * 128:kt * 128 + 128], h[:, kt * 128:kt * 128 + 128], ident[:, :]),
                    ("mt", kt), [("mh2", 0), ("c_id", 0), *free])
            put("act", lambda e: e.copy(hT[:, :, :].rearrange("p a b -> p (a b)"), bank2[:, :]), ("mhT", 0), [("mt", 3)])
            xp_free[s] = (("mhT", 0),)

        def mlp2():
            h, hT = P["h"], P["hT"]
            bank = ps["acc1"]
            zeros(bank, 1, [("mh", 0)])
            for i, (n, r, _) in enumerate(nets):
                for kt in range(4):
                    sl, c, key = load_chunk(A[n + "_w2"][kt])
                    put("pe", lambda e, r=r, kt=kt, c=c: mm(e, bank[r:r + 4, :], hT[:, kt, r:r + 4], c),
                        ("m2", i * 4 + kt), [key, ("mhT", 0)])
                    r_free[sl] = (("m2", i * 4 + kt),)
            cv = [load_chunk(A["rows_v"][j]) for j in (1, 2, 3)]
            put("dve", lambda e: e.tensor_tensor(h[:, :], bank[:, :], cv[0][1], ALU.add), ("mv0", 0), [("m2", 11), cv[0][2], ("mt", 3)])
            r_free[cv[0][0]] = (("mv0", 0),)
            bs = small[:, 8:14]
            mv = small[:, 14:16]
            put("dve", lambda e: e.bn_stats(bs, h[:, :]), ("mv1", 0), [("mv0", 0)])
            put("dve", lambda e: e.bn_aggr(mv, bs), ("mv2", 0), [("mv1", 0)])
            put("pool", lambda e: e.tensor_tensor(small[:, 16:17], mv[:, 1:2], eps5, ALU.add), ("mv3", 0), [("mv2", 0), ("c_eps", 0)])
            put("pool", lambda e: e.tensor_tensor(small[:, 17:18], small[:, 16:17], mh, ALU.pow), ("mv4", 0), [("mv3", 0), ("c_cst", 0)])
            put("dve", lambda e: e.tensor_scalar(h[:, :], h[:, :], mv[:, 0:1], small[:, 17:18], ALU.subtract, ALU.mult), ("mv5", 0), [("mv4", 0)])
            put("dve", lambda e: e.tensor_tensor(h[:, :], h[:, :], cv[1][1], ALU.mult), ("mv6", 0), [("mv5", 0), cv[1][2]])
            r_free[cv[1][0]] = (("mv6", 0),)
            put("dve", lambda e: e.tensor_tensor(h[:, :], h[:, :], cv[2][1], ALU.add), ("mv7", 0), [("mv6", 0), cv[2][2]])
            r_free[cv[2][0]] = (("mv7", 0),)
            s, bank2, free = xp_bank()
            for kt in range(4):
                put("pe", lambda e, kt=kt: e.transpose(bank2[:, kt * 128:kt * 128 + 128], h[:, kt * 128:kt * 128 + 128], ident[:, :]),
                    ("mu", kt), [("mv7", 0), *free])
            put("act", lambda e: e.copy(hT[:, :, :].rearrange("p a b -> p (a b)"), bank2[:, :]), ("vT", 0), [("mu", 3), ("m2", 11)])
            xp_free[s] = (("vT", 0),)

        spec = [("m", 2, "hT", 0, 4, 64), ("n", 3, "hT", 32, 4, 64), ("r", 4, "hT", 64, 4, 64),
                ("t", 1, "tabT", 32, 5, 0), ("s", 5, "tabT", 64, 3, 32), ("h", 0, "tabT", 0, 5, 0)]
        block_of = {"h": 0, "t": 1, "m": 2, "n": 3, "r": 4, "s": 5}
        Pp = ps["acc0"]

        def table_rows(j, slot, free):
            name, w, src, c0, n, base = spec[j]
            t = P[f"L{slot}"]
            put("dve", lambda e: e.memset(t[:, :, :], 0.0), ("lz", j), free)
            for rep in range(3):
                put("dve", lambda e, rep=rep: e.tensor_scalar(t[:, :, base + 8 * rep:base + n + 8 * rep], P[src][:, :, c0:c0 + n], w6[:, w:w + 1], None, ALU.mult),
                    ("lb", 3 * j + rep), [("lz", j), ("w6", 0), ("vT", 0) if src == "hT" else ("c_tabT", 0)])
            return t

        def w1_ths(j, free, start=False):
            name = spec[j][0]
            t = table_rows(j, j - 3, free)
            for kt in range(4):
                sl, c, key = load_chunk(A["int_w1"][block_of[name] * 4 + kt])
                put("pe", lambda e, kt=kt, c=c: mm(e, Pp[0:96, :], t[:, kt, :], c, start=(start and kt == 0)), ("Pm", (j - 3) * 4 + kt), [key, ("lb", 3 * j + 2)])
                rd = split_weight(c, [key], W1[name, "h"], W1[name, "l"], kt, ("dve", "pool")[kt % 2])
                r_free[sl] = (("Pm", (j - 3) * 4 + kt), *rd)
                w1_done[name] = [*w1_done.get(name, ()), *rd]

        def w1_x():
            Ls = [table_rows(j, j, [("Pm", 4 * j + 3)]) for j in range(3)]
            for kt in range(4):
                xacc = (P["h"], P["t1"])[kt % 2]
                for j in range(3):
                    name, w = spec[j][:2]
                    sl, c, key = load_chunk(A["int_w1"][block_of[name] * 4 + kt])
                    i = 12 + kt * 3 + j
                    put("pe", lambda e, j=j, kt=kt, c=c: mm(e, Pp[0:96, :], Ls[j][:, kt, :], c), ("Pm", i), [key, ("lb", 3 * j + 2)])
                    if j == 0:
                        put("dve", lambda e, c=c, w=w, xacc=xacc: e.tensor_scalar(xacc[:, :], c, w6[:, w:w + 1], None, ALU.mult), ("xa", 3 * kt), [key, ("mu", 3), ("s3_6", 3), *xfree[kt % 2]])
                    else:
                        put("dve", lambda e, c=c, w=w, xacc=xacc: e.scalar_tensor_tensor(out=xacc[:, :], in0=c, scalar=w6[:, w:w + 1], in1=xacc[:, :], op0=ALU.mult, op1=ALU.add),
                            ("xa", 3 * kt + j), [key, ("xa", 3 * kt + j - 1)])
                    r_free[sl] = (("Pm", i), ("xa", 3 * kt + j))
                xfree[kt % 2] = split_weight(xacc[:, :], [("xa", 3 * kt + 2)], W1["x", "h"], W1["x", "l"], kt, "pool")
                w1_done["x"] = [*w1_done.get("x", ()), *xfree[kt % 2]]

        def table_P():
            t0 = P["t0"]
            put("sp", lambda e: e.dma_start(t0[:, :], A["rows_p"]), ("pb", 0), [("s3_6", 3)], dma=True)
            put("dve", lambda e: e.tensor_tensor(t0[0:96, :], t0[0:96, :], Pp[0:96, :], ALU.add), ("pbs", 0), [("pb", 0), ("Pm", 23)])
            split3(t0[:, :], PT[:, :], 4, [("pbs", 0), *xfree[1]])

        xfree = [(), ()]
        w1_done = {}

        def load_x(g):
            put("sp", lambda e: e.dma_start(xraw[:, :, :], A["xT"][g]), ("ldx", g), [("xlo", g - 1), ("xhi", g - 1)], dma=True)

        def load_tok(g):
            s = g % 4
            put("sp", lambda e: e.dma_start(xb[s][:, :], A["x"][g * 128:g * 128 + 128, :]), (f"ldt{s}", g), [(f"out{s}", g - 4), *([("stt", s)] if s > 1 else [])], dma=True)

        def split_x(g):
            put("act", lambda e: e.copy(xhi[:, :, :], xraw[:, :, :]), ("xhi", g), [("ldx", g), ("A", g - 1)])
            put("pool", lambda e: e.tensor_tensor(xlo[:, :, :], xraw[:, :, :], xhi[:, :, :].bitcast(F32), ALU.subtract), ("xlo", g), [("xhi", g), ("ldx", g), ("A", g - 1)])

        qslot = {}

        def stage_A(g):
            s, bank, free = tok_bank()
            b = g // 8
            for kt in range(4):
                put("pe", lambda e, kt=kt: three(e, bank[:, :], xhi[:, kt, :], xlo[:, kt, :], WL["k", "h"][:, kt, :], WL["k", "l"][:, kt, :], kt == 0),
                    None, [("xhi", g), ("xlo", g), *mw_done[b, 0], *free])
            put("pe", lambda e: mm(e, bank[:, :], selT[:, 0, :], biasT[:, :]), ("A", g), [("c_sel", 0), ("s3_6", 0)])
            put("dve", lambda e: e.transpose(q[:, :].rearrange("p (t h) -> p h t", h=16), bank[:, :].rearrange("p (h t) -> p h t", h=16)),
                ("qT", g), [("A", g), ("q3", g - 1), ("q2", g - 1)])
            tok_free[s] = (("qT", g),)

        def stage_A1(g):
            put("act", lambda e: e.copy(q12[:, :, 0], q[:, :]), ("q1", g), [("qT", g), *q12_used(g)])
            put("pool", lambda e: e.tensor_tensor(q[:, :], q[:, :], q12[:, :, 0], ALU.subtract), ("qr", g), [("q1", g), ("qT", g)])

        def q12_used(g):
            return [("S", g - 1), ("VT", g - 1), ("bdq", g - 1)]

        def stage_A2(g):
            put("act", lambda e: e.copy(q12[:, :, 1], q[:, :]), ("q2", g), [("qr", g), *q12_used(g)])
            put("pool", lambda e: e.tensor_tensor(q3[:, :], q[:, :], q12[:, :, 1], ALU.subtract), ("q3", g), [("q2", g), ("S", g - 1), ("VT3", g - 1), ("bdq3", g - 1)])

        def stage_bdq(g):
            for i in range(4):
                r = slice(32 * i, 32 * i + 32)
                put("dve", lambda e, i=i, r=r: e.tensor_copy(BD12[r, :, i, :, :].rearrange("p g m t -> p g (m t)"), q12[r, :, :].rearrange("p (g m) t -> p g (m t)", g=16)),
                    ("bdq", g) if i == 3 else None, [("q1", g), ("q2", g), ("AV", g - 1), ("c_bd12", 0)])
            for i in range(4):
                r = slice(32 * i, 32 * i + 32)
                put("act", lambda e, i=i, r=r: e.copy(BD3[r, :, i, :], q3[r, :].rearrange("p (g m) -> p g m", g=16)),
                    ("bdq3", g) if i == 3 else None, [("q3", g), ("S", g - 1), ("c_bd3", 0)])

        def stage_V(g):
            put("dve", lambda e: e.transpose(v12[:, :, :].rearrange("p a b -> p (a b)").bitcast(U32), q12[:, :, :].rearrange("p a b -> p (a b)").bitcast(U32)),
                ("VT", g), [("q1", g), ("q2", g), ("AV", g - 1)])
            put("dve", lambda e: e.transpose(v3[:, :], q3[:, :]), ("VT3", g), [("q3", g), ("AV", g - 1)])

        mx, den, rden = small[:, 18:34], small[:, 34:50], small[:, 50:66]

        def by_head(t):
            return t[:, :].rearrange("p (g m) -> p g m", m=32)

        def stage_S(g):
            att = ps["att0"]

            def run(e, j):
                c = slice(j * 32, j * 32 + 32)
                o = att[:, c]
                w1 = BD12[:, j, :, :, 0].rearrange("p a b -> p (a b)")
                w2 = BD12[:, j, :, :, 1].rearrange("p a b -> p (a b)")
                w3 = BD3[:, j, :, :].rearrange("p a b -> p (a b)")
                r1, r2, r3 = q12[:, c, 0], q12[:, c, 1], q3[:, c]
                for a, b in ((w1, r1), (w1, r2), (w1, r3), (w2, r1), (w2, r2)):
                    mm(e, o, a, b)
                return mm(e, o, w3, r1)

            put("pe", lambda e: mm(e, att[:, :], maskL[:, :], maskR[:, :].unsqueeze(1).to_broadcast([128, 16, 32]), start=True), None,
                [("sub", g - 1), ("c_mL", 0), ("c_mR", 0)])
            for j in range(16):
                put("pe", lambda e, j=j: run(e, j), ("S", g) if j == 15 else None, [("bdq", g), ("bdq3", g), ("q3", g)])
            v = by_head
            put("dve", lambda e: e.tensor_reduce(mx, v(att), axis=AX.X, op=ALU.max), ("mx", g), [("S", g), ("sub", g - 1)])
            put("dve", lambda e: e.tensor_tensor(v(SE), v(att), mx.unsqueeze(2).to_broadcast([128, 16, 32]), ALU.subtract),
                ("sub", g), [("mx", g), ("aTr", g - 1), ("sty", 1)])
            put("act", lambda e: e.activation(SE[:, :], SE[:, :], ACT.Exp, scale=SCALE), ("exp", g), [("sub", g)])

        def stage_E(g):
            v = by_head
            put("dve", lambda e: e.transpose(ET[:, :], SE[:, :]), ("ET", g), [("exp", g), ("nT2", g - 1), ("sty", 1)])
            put("act", lambda e: e.copy(e12[:, :, 0], ET[:, :]), ("e1", g), [("ET", g), ("bde", g - 1)])
            put("dve", lambda e: e.tensor_reduce(den, v(SE), axis=AX.X, op=ALU.add), ("den", g), [("exp", g)])
            put("dve", lambda e: e.tensor_tensor(e12[:, :, 1], ET[:, :], e12[:, :, 0], ALU.subtract), ("e2", g), [("e1", g), ("ET", g), ("bde", g - 1)])
            put("dve", lambda e: e.reciprocal(rden, den), ("rden", g), [("den", g), ("norm", g - 1)])
            for i in range(4):
                r = slice(32 * i, 32 * i + 32)
                put("dve", lambda e, i=i, r=r: e.tensor_copy(BD12[r, :, i, :, :].rearrange("p g m t -> p g (m t)").bitcast(F16), e12[r, :, :].rearrange("p (g m) t -> p g (m t)", g=16)),
                    ("bde", g) if i == 3 else None, [("e1", g), ("e2", g), ("S", g)])

        def stage_AV(g):
            att = ps["att1"]

            def run(e, j):
                c = slice(j * 32, j * 32 + 32)
                o = att[:, c]
                w1 = BD12[:, j, :, :, 0].rearrange("p a b -> p (a b)").bitcast(F16)
                w2 = BD12[:, j, :, :, 1].rearrange("p a b -> p (a b)").bitcast(F16)
                mm(e, o, w1, v12[:, c, 0], start=(j == 0))
                mm(e, o, w1, v12[:, c, 1])
                mm(e, o, w1, v3[:, c])
                mm(e, o, w2, v12[:, c, 0])
                return mm(e, o, w2, v12[:, c, 1])

            for j in range(16):
                put("pe", lambda e, j=j: run(e, j), ("AV", g) if j == 15 else None, [("bde", g), ("VT", g), ("VT3", g), ("norm", g - 1)])
            v = by_head
            put("dve", lambda e: e.tensor_tensor(v(SE), v(att), rden.unsqueeze(2).to_broadcast([128, 16, 32]), ALU.mult), ("norm", g), [("AV", g), ("rden", g), ("den", g), ("ET", g)])
            put("dve", lambda e: e.transpose(ET[:, :].rearrange("p (h g t) -> p g t h", h=16, t=2), SE[:, :]), ("nT", g), [("norm", g), ("e1", g), ("e2", g)])
            put("dve", lambda e: e.transpose(SE[:, :], ET[:, :]), ("nT2", g), [("nT", g)])

        def stage_aTr(g):
            s, bank, free = xp_bank()
            for c in range(4):
                put("pe", lambda e, c=c: e.transpose(bank[:, c * 128:c * 128 + 128], SE[:, c * 128:c * 128 + 128], ident[:, :]),
                    ("aTr", g) if c == 3 else None, [("nT2", g), ("c_id", 0), *free])
            v = bank[:, :].rearrange("p (c t) -> p c t", c=4)
            put("act", lambda e: e.copy(ahi[:, :, :], v), ("ahi", g), [("aTr", g), ("O", g - 1)])
            av_bank[g] = s, v

        av_bank = {}

        def stage_alo(g):
            s, v = av_bank[g]
            put("dve", lambda e: e.tensor_tensor(alo[:, :, :], v, ahi[:, :, :].bitcast(F32), ALU.subtract), ("alo", g), [("ahi", g), ("O", g - 1)])
            xp_free[s] = (("alo", g),)

        st1, mv1, rs1 = small[:, 66:72], small[:, 72:74], small[:, 74:76]
        st2_, mv2, rs2 = small[:, 76:82], small[:, 82:84], small[:, 84:86]
        st3, mv3, rs3 = small[:, 86:92], small[:, 92:94], small[:, 94:96]

        def stage_O(g):
            s, bank, free = tok_bank()
            b = g // 8
            xs = xb[g % 4]
            for kt in range(4):
                put("pe", lambda e, kt=kt: three(e, bank[:, :], ahi[:, kt, :], alo[:, kt, :], WL["o", "h"][:, kt, :], WL["o", "l"][:, kt, :], kt == 0),
                    None, [("ahi", g), ("alo", g), *mw_done[b, 1], *free])
            put("pe", lambda e: mm(e, bank[:, :], selT[:, 1, :], biasT[:, :]), ("O", g), [])
            put("dve", lambda e: e.tensor_tensor(xs[:, :], bank[:, :], xs[:, :], ALU.add), ("x1", g), [("O", g), (f"ldt{g % 4}", g)])
            tok_free[s] = (("x1", g),)
            put("dve", lambda e: e.bn_stats(st1, xs[:, :]), ("b1", g), [("x1", g)])
            put("dve", lambda e: e.bn_aggr(mv1, st1), ("a1", g), [("b1", g), ("z", g - 1)])
            put("pool", lambda e: e.tensor_tensor(rs1[:, 0:1], mv1[:, 1:2], eps5, ALU.add), ("r1a", g), [("a1", g), ("c_eps", 0), ("r1", g - 1)])
            put("pool", lambda e: e.tensor_tensor(rs1[:, 1:2], rs1[:, 0:1], mh, ALU.pow), ("r1", g), [("r1a", g), ("z", g - 1), ("c_cst", 0)])

        def stage_z(g):
            xs = xb[g % 4]
            put("dve", lambda e: e.tensor_scalar(z[:, :], xs[:, :], mv1[:, 0:1], rs1[:, 1:2], ALU.subtract, ALU.mult), ("z", g), [("r1", g), ("zTr", g - 1), ("v1", g - 1), ("stt", 6)])

        def stage_v(g):
            pg, pb = pgb[:, 0:512], pgb[:, 512:1024]
            put("pool", lambda e: e.tensor_tensor(pg, z[:, :], pg, ALU.mult), ("v1", g), [("z", g), ("gat", g)])
            put("pool", lambda e: e.tensor_tensor(pg, pg, pb, ALU.add), ("v2", g), [("v1", g)])

        def stage_v2(g):
            pg = pgb[:, 0:512]
            put("dve", lambda e: e.bn_stats(st2_, pg), ("b2", g), [("v2", g)])
            put("dve", lambda e: e.bn_aggr(mv2, st2_), ("a2", g), [("b2", g), ("u", g - 1)])
            put("pool", lambda e: e.tensor_tensor(rs2[:, 0:1], mv2[:, 1:2], eps5, ALU.add), ("r2a", g), [("a2", g), ("r2", g - 1)])
            put("pool", lambda e: e.tensor_tensor(rs2[:, 1:2], rs2[:, 0:1], mh, ALU.pow), ("r2", g), [("r2a", g), ("u", g - 1)])

        def stage_u(g):
            pg = pgb[:, 0:512]
            put("dve", lambda e: e.tensor_scalar(pg, pg, mv2[:, 0:1], rs2[:, 1:2], ALU.subtract, ALU.mult), ("u", g), [("r2", g), ("v2", g)])

        def gather(g):
            off = bass.IndirectOffsetOnAxis(ap=pidx[:, g:g + 1].bitcast(U32), axis=0)
            put("pool", lambda e: e.indirect_dma_start(pgb[:, :], None, A["pw"], off), ("gat", g), [("uTr", g - 1), ("v2", g - 1), ("c_pidx", 0), ("stt", 5)], dma=True)

        def xpose(g, src, needs, key):
            s, bank, free = xp_bank()
            for c in range(4):
                put("pe", lambda e, c=c: e.transpose(bank[:, c * 128:c * 128 + 128], src[:, c * 128:c * 128 + 128], ident[:, :]),
                    key if c == 3 else None, [*needs, ("c_id", 0), *free])
            return s, bank[:, :].rearrange("p (c t) -> p c t", c=4)

        def half(g):
            return slice((g % 2) * 128, (g % 2) * 128 + 128)

        def stage_x1T(g):
            k = g // 2
            s, v = xpose(g, xb[g % 4], [("x1", g)], ("xTr", g))
            h = half(g)
            put("act", lambda e: e.copy(op[0]["h"][:, :, h], v), ("oxh", g), [("xTr", g), ("W2", 2 * k - 1), *pro_end])
            xt[g] = s, v, h

        xt = {}

        def stage_x1T2(g):
            s, v, h = xt[g]
            k = g // 2
            put("dve", lambda e: e.tensor_tensor(op[0]["l"][:, :, h], v, op[0]["h"][:, :, h].bitcast(F32), ALU.subtract), ("oxl", g), [("oxh", g), ("W2", 2 * k - 1)])
            xp_free[s] = (("oxl", g),)
            put("pool", lambda e: e.tensor_tensor(xb[g % 4][:, :], xb[g % 4][:, :], beint[:, :], ALU.add), ("xbe", g), [("xTr", g), ("z", g), ("b1", g), ("c_be", 0)])

        def stage_zT(g):
            s, v = xpose(g, z, [("z", g)], ("zTr", g))
            put("act", lambda e: e.copy(zT[:, :, half(g)], v), ("zT", g), [("zTr", g), ("prod_s", g - 2), ("prod_t", g - 2), *pro_end])
            xp_free[s] = (("zT", g),)

        def stage_uT(g):
            s, v = xpose(g, pgb, [("u", g)], ("uTr", g))
            put("act", lambda e: e.copy(uT[:, :, :], v), ("uT", g), [("uTr", g), ("prod_h", g - 1), *pro_end])
            xp_free[s] = (("uT", g),)

        def one_hot(k):
            s = k % 2
            used = [("W1x1", k - 2), ("Gs", 2 * k - 3), ("Gh", 2 * k - 3)]
            rd = [("oh", k - 1)]
            t = slice(k * 256, k * 256 + 256)
            for i, nm in enumerate(("cid", "sid", "bid")):
                put("sp", lambda e, i=i, nm=nm: e.dma_start(ids[32 * i:32 * i + 32, :], A[nm][t].partition_broadcast(32)),
                    ("ids", k * 3 + i), [*rd, ("c_ids", 0)], dma=True)
            put("dve", lambda e: e.tensor_scalar(OH[s][:, :], ids[:, :], cst[:, 0:1], None, ALU.is_equal), ("oh", k), [("ids", k * 3 + 2), ("c_cst", 0), *used])

        def product(g, name):
            k = g // 2
            s, bank, free = xp_bank()
            tab = GT[name]
            nG = {"t": 0, "s": 1, "h": 2}[name]
            for c in range(4):
                put("pe", lambda e, c=c: mm(e, bank[:, c * 128:c * 128 + 128], tab[:, c * 128:c * 128 + 128], OH[k % 2][:, half(g)], start=(c == 0)),
                    ("G" + name, g) if c == 3 else None, [("oh", k), ("s3_6", 1 + nG), *free])
            pr[name, g] = s, bank

        pr = {}

        def product2(g, name, src, srckey, slot, freekeys):
            s, bank = pr[name, g]
            ys, y, yf = y_buf()
            yv = y[:, :].rearrange("p (c t) -> p c t", c=4)
            put("dve", lambda e: e.tensor_tensor(yv, src, bank[:, :].rearrange("p (c t) -> p c t", c=4), ALU.mult), ("prod_" + name, g), [("G" + name, g), srckey, *yf])
            xp_free[s] = (("prod_" + name, g),)
            h = half(g)
            put("act", lambda e: e.copy(op[slot]["h"][:, :, h], yv), (f"o{name}h", g), [("prod_" + name, g), *freekeys])
            put("pool", lambda e: e.tensor_tensor(op[slot]["l"][:, :, h], yv, op[slot]["h"][:, :, h].bitcast(F32), ALU.subtract), (f"o{name}l", g), [(f"o{name}h", g), *freekeys])
            y_free[ys] = ((f"o{name}l", g),)

        def stage_t(g):
            product2(g, "t", zT[:, :, half(g)], ("zT", g), 1, [("W1h1", g // 2 - 1)])

        def stage_s(g):
            product2(g, "s", zT[:, :, half(g)], ("zT", g), 0, [("W1x1", g // 2)])

        def stage_h(g):
            product2(g, "h", uT[:, :, :], ("uT", g), 1, [("W1t1", g // 2)])

        slot_of = {"x": 0, "t": 1, "s": 0, "h": 1}

        def stage_W1(k, name, pair):
            acc = ps[f"acc{pair}"]
            o = op[slot_of[name]]
            needs = [(f"o{name}h", 2 * k + 1), (f"o{name}l", 2 * k + 1), *w1_done[name]]
            for j in range(2):
                m = 2 * pair + j
                dst = acc[:, j * 256:j * 256 + 256]
                ms = slice(m * 128, m * 128 + 128)
                if name == "x":
                    put("pe", lambda e, j=j, dst=dst, ms=ms: mm(e, dst, PT[:, ms], OH[k % 2][:, :], start=(j == 0)), None,
                        [("sil", 2 * (k - 1) + pair), ("oh", k), ("s3_6", 4), ("mv0", 0)])
                for kt in range(4):
                    put("pe", lambda e, kt=kt, dst=dst, ms=ms: three(e, dst, W1[name, "h"][:, kt, ms], W1[name, "l"][:, kt, ms], o["h"][:, kt, :], o["l"][:, kt, :], False),
                        (f"W1{name}{pair}", k) if (j == 1 and kt == 3) else None, needs)

        def stage_silu(k, pair):
            ys, y, yf = y_buf()
            n = 2 * k + pair
            acc = ps[f"acc{pair}"]
            c = slice(2 * pair, 2 * pair + 2)
            put("act", lambda e: e.activation(y[:, :], acc[:, :], ACT.Silu), ("sil", n), [(f"W1h{pair}", k), *yf])
            hv = lambda p: op[0][p][:, c, :].rearrange("p a b -> p (a b)")
            put("act", lambda e: e.copy(hv("h"), y[:, :]), ("ash", n), [("sil", n), ("W1s1", k)])
            sil[n] = ys, y, hv

        sil = {}

        def stage_silu2(k, pair):
            n = 2 * k + pair
            ys, y, hv = sil[n]
            put("dve", lambda e: e.tensor_tensor(hv("l"), y[:, :], hv("h").bitcast(F32), ALU.subtract), ("asl", n), [("ash", n), ("W1s1", k)])
            y_free[ys] = (("asl", n),)

        def stage_W2(g):
            k = g // 2
            s, bank, free = tok_bank()
            for m in range(4):
                put("pe", lambda e, m=m: three(e, bank[:, :], op[0]["h"][:, m, half(g)], op[0]["l"][:, m, half(g)], WL["2", "h"][:, m, :], WL["2", "l"][:, m, :], m == 0),
                    None, [("ash", 2 * k + 1), ("asl", 2 * k + 1), *w2_done[0], *free])
            put("pe", lambda e: mm(e, bank[:, :], selT[:, 2, :], biasT[:, :]), ("W2", g), [])
            put("dve", lambda e: e.bn_stats(st3, bank[:, :]), ("b3", g), [("W2", g)])
            put("dve", lambda e: e.bn_aggr(mv3, st3), ("a3", g), [("b3", g), ("w", g - 1)])
            put("pool", lambda e: e.tensor_tensor(rs3[:, 0:1], mv3[:, 1:2], eps5, ALU.add), ("r3a", g), [("a3", g), ("r3", g - 1)])
            put("pool", lambda e: e.tensor_tensor(rs3[:, 1:2], rs3[:, 0:1], mh, ALU.pow), ("r3", g), [("r3a", g), ("fin", g - 1)])
            ys, y, yf = y_buf()
            put("dve", lambda e: e.scalar_tensor_tensor(out=y[:, :], in0=bank[:, :], scalar=mv3[:, 0:1], in1=gint[:, :], op0=ALU.subtract, op1=ALU.mult),
                ("w", g), [("a3", g), ("c_gi", 0), *yf])
            tok_free[s] = (("w", g),)
            w_tile[g] = ys, y

        w_tile = {}

        def stage_out(g):
            xs = xb[g % 4]
            ys, y = w_tile[g]
            put("dve", lambda e: e.scalar_tensor_tensor(out=xs[:, :], in0=y[:, :], scalar=rs3[:, 1:2], in1=xs[:, :], op0=ALU.mult, op1=ALU.add),
                ("fin", g), [("w", g), ("r3", g), ("xbe", g)])
            y_free[ys] = (("fin", g),)
            put("sp", lambda e: e.dma_start(out[g * 128:g * 128 + 128, :], xs[:, :]), (f"out{g % 4}", g), [("fin", g)], dma=True)

        pro_end = []

        consts()
        style(0)
        demodulation(0)
        load_x(0)
        consts2()
        bias_table()
        mod_weights(0, 0)
        split_x(0)
        style(1)
        demodulation(1)
        stage_A(0)
        stage_A1(0)
        stage_A2(0)
        load_x(1)
        slots.extend(w_slots[0][0:2])
        weights_softmax()
        stage_bdq(0)
        stage_V(0)
        split_x(1)
        mod_weights(0, 1)
        for g in range(4):
            load_tok(g)
        one_hot(0)

        for k in range(NT + 1):
            a, b = 2 * k, 2 * k + 1
            pa, pb = a - 2, a - 1
            front, back, more = k < NT, k > 0, k < NT - 1
            if front:
                stage_S(a)
                if back:
                    stage_x1T(pb)
                stage_A(b)
                stage_A1(b)
                if back:
                    stage_x1T2(pb)
                stage_E(a)
                stage_A2(b)
                if more:
                    load_x(a + 2)
            else:
                stage_x1T(pb)
                stage_x1T2(pb)
            if back:
                stage_zT(pb)
                stage_v(pb)
                stage_W1(k - 1, "x", 0)
                product(pb, "t")
                stage_t(pb)
                stage_v2(pb)
                stage_W1(k - 1, "x", 1)
                stage_u(pb)
                product(pa, "s")
                stage_s(pa)
            else:
                mlp1()
                g_table(0)
            if front:
                stage_AV(a)
            if back:
                product(pb, "s")
                stage_s(pb)
                stage_W1(k - 1, "t", 0)
            if front:
                stage_aTr(a)
                stage_bdq(b)
                stage_alo(a)
                if more:
                    split_x(a + 2)
                    load_x(b + 2)
                stage_V(b)
                if k:
                    one_hot(k)
                if a % 8 == 0 and k:
                    mod_weights(a // 8, 1)
            if back:
                stage_W1(k - 1, "t", 1)
                product(pa, "h")
                stage_h(pa)
            if front:
                stage_O(a)
            if back:
                stage_uT(pb)
            if front:
                gather(a)
            if back:
                product(pb, "h")
                stage_h(pb)
            if front:
                stage_z(a)
                stage_v(a)
                if more:
                    if (a + 2) % 8 == 0:
                        mod_weights((a + 2) // 8, 0)
                    stage_A(a + 2)
            if not back:
                w1_ths(3, [], start=True)
                mlp2()
            if front:
                stage_S(b)
                stage_v2(a)
                if more:
                    stage_A1(a + 2)
            if back:
                stage_W1(k - 1, "s", 0)
            if front:
                stage_E(b)
                stage_u(a)
                if more:
                    stage_A2(a + 2)
                    split_x(b + 2)
            if back:
                stage_W1(k - 1, "s", 1)
            if not back:
                w1_ths(4, [])
                w1_ths(5, [("mz", 1)])
                g_table(1)
                g_table(2)
                w1_x()
                table_P()
                w2_weights()
                pro_end.extend([("Pm", 23), ("s3_6", 4), ("wl", nw[0] - 1), ("wh", nw[0] - 1), ("wl", nw[0] - 2), *r_free["cr0"], *r_free["cr1"], ("dmp", 1)])
                del slots[2:]
            if front:
                stage_zT(a)
                stage_uT(a)
                gather(b)
            if back:
                stage_W1(k - 1, "h", 0)
                stage_silu(k - 1, 0)
                stage_silu2(k - 1, 0)
                stage_W1(k - 1, "h", 1)
                stage_silu(k - 1, 1)
                stage_silu2(k - 1, 1)
            if front:
                stage_AV(b)
                product(a, "t")
                stage_t(a)
            if back:
                stage_W2(pa)
                stage_out(pa)
            if front:
                stage_aTr(b)
                stage_alo(b)
                if more:
                    stage_bdq(a + 2)
            if back:
                stage_W2(pb)
                stage_out(pb)
                if more:
                    load_tok(a + 2)
                    load_tok(b + 2)
            if front:
                if more:
                    stage_V(a + 2)
                stage_O(b)
                stage_x1T(a)
                stage_x1T2(a)
                stage_z(b)
        for s in range(4):
            put("sp", None, None, [(f"out{s}", NG - 4 + s)])

        sems = {n: ctx.enter_context(nc.semaphore("s_" + n)) for n in Q.count}
        block = ctx.enter_context(nc.Block())

        @block.sync
        def _(e):
            Q.emit("sp", e, sems)

        @block.tensor
        def _(e):
            Q.emit("pe", e, sems)

        @block.scalar
        def _(e):
            Q.emit("act", e, sems)

        @block.vector
        def _(e):
            Q.emit("dve", e, sems)

        @block.gpsimd
        def _(e):
            Q.emit("pool", e, sems)


NAMES = ["cond_512", "cond_64", "fside_Bx32_0"]


def kernel(**inp):
    import ml_dtypes
    import concourse.bacc as bacc
    from concourse.bass_utils import run_bass_kernel_spmd

    bf = ml_dtypes.bfloat16
    get = lambda n: np.asarray(inp[n])
    c = lambda x: np.ascontiguousarray(x)
    L0 = lambda n: get("L0_cond_" + n)
    L1 = lambda n: get("L1_cond_" + n)
    x = get("x").reshape(4096, 512)
    arr = {"x": c(x), "xT": c(x.reshape(NG, 128, 4, 128).transpose(0, 3, 2, 1))}

    def blocks(w, rows=None):
        n = w.shape[0]
        m = -(-n // 128)
        o = np.zeros((m * 128, w.shape[1]), w.dtype)
        o[:n] = w
        return c(o.reshape(m, 128, w.shape[1]))

    for s in "ko":
        arr[s + "_affT"] = blocks(L0(s + "_aff_w").T)
        arr[s + "_wT"] = blocks(L0(s + "_w").T)
    arr["affb"] = c(np.stack([L0("k_aff_b").reshape(4, 128).T, L0("o_aff_b").reshape(4, 128).T], 1))
    cond = np.zeros((4, 128, 4), np.float32)
    cond[0:2] = get("cond_512").T.reshape(2, 128, 4)
    cond[2, 0:64] = get("cond_64").T
    cond[3, 0:32] = get("fside_Bx32_0").T
    arr["condT"] = c(cond.transpose(1, 0, 2))

    def rows(*placed, times=3):
        o = np.zeros((128, 512), np.float32)
        for r, a in placed:
            a = a.reshape(-1, 512)
            for j in range(times):
                o[r + 8 * j:r + 8 * j + len(a)] = a
        return o

    arr["rows_b"] = rows((0, L0("k_b")), (32, L0("o_b")), (64, L1("int_b2")))
    arr["rows_t"], arr["rows_s"], arr["rows_h"] = rows((0, L1("tm_g"))), rows((32, L1("ms_g"))), rows((0, L1("cp_g")))
    arr["rows_p"] = rows((64, np.tile(L1("int_b1"), (4, 1))))
    arr["rows_v"] = np.stack([rows(*[(32 * i, np.tile(L1(n + t), (4, 1))) for i, n in enumerate(("mem", "noi", "res"))], times=1)
                              for t in ("_b1", "_b2", "_g", "_be")])
    tab = rows((0, L1("cp_b")), (32, L1("tm_b")), (64, L1("ms_b")), times=1)
    arr["tabT"] = c(tab.T.reshape(4, 128, 128).transpose(1, 0, 2))
    arr["pw"] = c(np.concatenate([L1("pw_g"), L1("pw_b")], 1))
    for n in ("int_g", "int_be", "aw"):
        arr[n] = c(L1(n))
    for n in ("mem", "noi", "res"):
        arr[n + "_w1"] = blocks(L1(n + "_W1"))
        arr[n + "_w2"] = blocks(L1(n + "_W2"))
    arr["int_w1"] = blocks(L1("int_W1"))
    arr["int_w2"] = blocks(L1("int_W2"))
    arr["cid"] = c(get("itok_BxS_0_4").reshape(-1))
    arr["sid"] = c(get("mask_BxS_ik0").reshape(-1))
    arr["pidx"] = c(get("itok_BxS_0_999").reshape(NG, 128).T)
    arr["bid"] = np.repeat(np.arange(4, dtype=np.int32), 1024)
    p = np.arange(128)
    cst = np.zeros((128, 5), np.float32)
    n_of = {0: 5, 1: 3, 2: 4, 3: 0}
    cst[:, 0] = [(i % 8) if (i % 32) < 24 and (i % 8) < n_of[i // 32] else -1 for i in p]
    for j in range(3):
        cst[:, 1 + j] = (p % 32) // 8 == j
    cst[:, 4] = -0.5
    arr["cst"] = cst
    arr["ident"] = np.eye(128, dtype=np.float32)
    arr["selT"] = c(np.broadcast_to((p[:, None] // 32 == np.arange(3)[None])[:, :, None], (128, 3, 128)).astype(bf))
    t2 = (p % 32) // 16
    arr["maskL"] = (np.where(p[:, None] == t2[None], np.float32(NEG), np.float32(0))).astype(bf)
    m = np.arange(32) // 16
    arr["maskR"] = ((p[:, None] != m[None]) & (p[:, None] < 2)).astype(bf)

    nc = bacc.Bacc("TRN2", target_bir_lowering=False, num_devices=1)
    A = {n: nc.dram_tensor("in_" + n, a.shape, mybir.dt.from_np(a.dtype), kind="ExternalInput").ap() for n, a in arr.items()}
    out = nc.dram_tensor("out", (4096, 512), F32, kind="ExternalOutput").ap()
    build(nc, A, out)
    r = run_bass_kernel_spmd(nc, [{"in_" + n: a for n, a in arr.items()}], core_ids=[0])
    return r.results[0]["out"].reshape(4, 1024, 512)
```

```python
import numpy as np
import concourse.bass as bass
from concourse import mybir
from contextlib import ExitStack

F32 = mybir.dt.float32
F32R = mybir.dt.float32r
BF16 = mybir.dt.bfloat16
F16 = mybir.dt.float16
I32 = mybir.dt.int32
U32 = mybir.dt.uint32
ALU = mybir.AluOpType
ACT = mybir.ActivationFunctionType
AX = mybir.AxisListType

NG = 32
NT = 16
SCALE = 32.0 ** -0.5
NEG = -1.0e30

PROLOGUE = set("""c_eps c_z c_bd12 c_bd3 c_ids sty styl stsq wsq dmm dme dmp s3_0 s3_1 s3_2 s3_3 s3_4 s3_5
s3_6 wm ws we wd wr w6 gw mz m1 mh mh2 mt mhT m2 mv0 mv1 mv2 mv3 mv4 mv5 mv6 mv7 mu vT lz lb Pm xa wh wl
pbs""".split())


class Queues:

    def __init__(self):
        self.items = {e: [] for e in ("pe", "act", "dve", "pool", "sp")}
        self.count = {}
        self.value = {}
        self.owner = {}

    def put(self, eng, fn, key=None, needs=(), dma=False):
        waits = []
        for n in needs:
            if n is not None and n[1] >= 0:
                waits.append(self.value[n])
        inc = None
        if key is not None:
            step = 16 if dma else 1
            name = "pro_" + eng if key[0] in PROLOGUE else key[0]
            assert self.owner.setdefault(name, eng) == eng, key
            self.count[name] = self.count.get(name, 0) + step
            self.value[key] = (name, self.count[name])
            inc = (name, step)
        self.items[eng].append((waits, fn, inc))

    def emit(self, eng, e, sems):
        seen = {}
        for waits, fn, inc in self.items[eng]:
            for stage, v in waits:
                if seen.get(stage, 0) < v:
                    e.wait_ge(sems[stage], v)
                    seen[stage] = v
            if fn is None:
                continue
            i = fn(e)
            if inc:
                i.then_inc(sems[inc[0]], inc[1])


def build(nc, A, out):
    Q = Queues()
    put = Q.put
    ctx = ExitStack()
    with ctx:
        def sb(name, shape, dt=F32, c=ctx):
            return c.enter_context(nc.sbuf_tensor(name, shape, dt))

        ident = sb("ident", [128, 128])
        cst = sb("cst", [128, 5])
        selT = sb("selT", [128, 3, 128], BF16)
        maskL = sb("maskL", [128, 128], BF16)
        maskR = sb("maskR", [128, 32], BF16)
        gint = sb("gint", [128, 512])
        beint = sb("beint", [128, 512])
        biasT = sb("biasT", [128, 512], BF16)
        GT = {n: sb("G" + n, [128, 512], BF16) for n in "ths"}
        PT = sb("PT", [128, 512], BF16)
        w6 = sb("w6", [128, 6])
        styl = sb("styl", [128, 2, 4, 4])
        dmT = sb("dmT", [128, 2, 16])
        pidx = sb("pidx", [128, NG], I32)
        W1 = {(n, p): sb(f"W1{n}{p}", [128, 4, 512], F32R) for n in "xtsh" for p in "hl"}
        WL = {(n, p): sb(f"W{n}{p}", [128, 4, 512], F32R) for n in ("k", "o", "2") for p in "hl"}
        NRING = 2
        ring = [sb(f"ring{i}", [128, 512])[:, :] for i in range(NRING)]
        ytmp = [sb(f"ytmp{i}", [128, 512]) for i in range(2)]
        small = sb("small", [128, 96])
        eps5 = small[:, 0:1]
        mh = cst[:, 4:5]

        ids = sb("ids", [128, 256], I32)
        OH = [sb(f"OH{i}", [128, 256], BF16) for i in range(2)]
        xraw = sb("xraw", [128, 4, 128])
        xhi = sb("xhi", [128, 4, 128], F32R)
        xlo = sb("xlo", [128, 4, 128], F32R)
        q = sb("q", [128, 512])
        q12 = sb("q12", [128, 512, 2], BF16)
        q3 = sb("q3", [128, 512], BF16)
        v12 = sb("v12", [128, 512, 2], BF16)
        v3 = sb("v3", [128, 512], BF16)
        BD12 = sb("BD12", [128, 16, 4, 32, 2], BF16)
        BD3 = sb("BD3", [128, 16, 4, 32], BF16)
        SE = sb("SE", [128, 512])
        ET = sb("ET", [128, 512])
        e12 = sb("e12", [128, 512, 2], F16)
        ahi = sb("ahi", [128, 4, 128], F32R)
        alo = sb("alo", [128, 4, 128], F32R)
        xb = [sb(f"xb{i}", [128, 512]) for i in range(4)]
        ps = {n: ctx.enter_context(nc.psum_tensor(n, [128, 512], F32))
              for n in ("acc0", "acc1", "tok0", "tok1", "xp0", "xp1")}
        att = ctx.enter_context(nc.psum_tensor("att", [128, 1024], F32))
        main = ExitStack()
        pro = ExitStack()
        with pro:
            psb = lambda n, s, d=F32: sb(n, s, d, pro)
            P = dict(
                h=psb("p_h", [128, 512]), hT=psb("p_hT", [128, 4, 128]),
                L0=psb("p_L0", [128, 4, 96]), L1=psb("p_L1", [128, 4, 96]), L2=psb("p_L2", [128, 4, 96]),
                t0=psb("p_t0", [128, 512]), t1=psb("p_t1", [128, 512]), t2=psb("p_t2", [128, 512]),
                tabT=psb("p_tabT", [128, 4, 128]),
                condT=psb("p_condT", [128, 4, 4]), abc=psb("p_abc", [128, 2, 4]),
                aw=psb("p_aw", [128, 6]), st2=psb("p_st2", [128, 2, 4, 4]), v=psb("p_v", [128, 2, 16]),
                r0=psb("p_r0", [128, 512]), r1=psb("p_r1", [128, 512]),
            )
        ctx.enter_context(main)
        msb = lambda n, s, d=F32: sb(n, s, d, main)
        op = [{p: msb(f"op{i}{p}", [128, 4, 256], F32R) for p in "hl"} for i in range(2)]
        zT = msb("zT", [128, 4, 256])
        uT = msb("uT", [128, 4, 128])
        z = sb("z", [128, 512])
        pgb = sb("pgb", [128, 1024])
        dmb = sb("dmb", [128, 512])

        tok_n = [0]
        tok_free = [(), ()]
        xp_n = [0]
        xp_free = [(), ()]

        def tok_bank():
            s = tok_n[0] % 2
            tok_n[0] += 1
            free, tok_free[s] = tok_free[s], None
            return s, ps[f"tok{s}"], free

        def xp_bank():
            s = xp_n[0] % 2
            xp_n[0] += 1
            free, xp_free[s] = xp_free[s], None
            return s, ps[f"xp{s}"], free

        y_n = [0]
        y_free = [(), ()]

        def y_buf():
            s = y_n[0] % 2
            y_n[0] += 1
            free, y_free[s] = y_free[s], None
            return s, ytmp[s], free

        slots = [(f"ring{i}", t) for i, t in enumerate(ring)]
        r_n = [0]
        r_free = {}
        r_use = {}

        def load_chunk(src, slot=None):
            if slot is None:
                slot = slots[r_n[0] % len(slots)]
                r_n[0] += 1
            name, t = slot
            n = r_use[name] = r_use.get(name, -1) + 1
            free, r_free[name] = r_free.get(name, ()), None
            put("sp", lambda e: e.dma_start(t, src), (name, n), free, dma=True)
            return name, t, (name, n)

        def mm(e, o, a, b, start=False):
            return e.matmul(o, a, b, start=start, stop=True, skip_group_check=True)

        def three(e, o, ah, al, bh, bl, start):
            mm(e, o, ah, bh, start)
            mm(e, o, ah, bl)
            return mm(e, o, al, bh)

        def consts():
            put("sp", lambda e: e.dma_start(P["condT"][:, :, :], A["condT"]), ("c_cond", 0), dma=True)
            put("act", lambda e: e.dma_start(P["abc"][:, :, :], A["affb"]), ("c_abc", 0), dma=True)
            put("act", lambda e: e.dma_start(cst[:, :], A["cst"]), ("c_cst", 0), dma=True)
            put("act", lambda e: e.dma_start(ident[:, :], A["ident"]), ("c_id", 0), dma=True)
            put("act", lambda e: e.dma_start(P["t0"][:, :], A["rows_b"]), ("c_rb", 0), dma=True)
            put("act", lambda e: e.dma_start(selT[:, :, :], A["selT"]), ("c_sel", 0), dma=True)
            put("dve", lambda e: e.memset(eps5, 1e-5), ("c_eps", 0))
            put("dve", lambda e: e.memset(P["L2"][:, :, :], 0.0), ("c_z", 0))
            put("pool", lambda e: e.memset(BD12[:, :, :, :, :].bitcast(U32), 0), ("c_bd12", 0))
            put("pool", lambda e: e.memset(BD3[:, :, :, :].bitcast(U32), 0), ("c_bd3", 0))
            put("pool", lambda e: e.memset(ids[:, :], 0), ("c_ids", 0))

        def consts2():
            put("act", lambda e: e.dma_start(maskL[:, :], A["maskL"]), ("c_mL", 0), dma=True)
            put("act", lambda e: e.dma_start(maskR[:, :], A["maskR"]), ("c_mR", 0), dma=True)
            put("act", lambda e: e.dma_start(P["aw"][:, :], A["aw"].partition_broadcast(128)), ("c_aw", 0), dma=True)
            put("act", lambda e: e.dma_start(pidx[:, :], A["pidx"]), ("c_pidx", 0), dma=True)
            put("act", lambda e: e.dma_start(P["tabT"][:, :, :], A["tabT"]), ("c_tabT", 0), dma=True)

        def consts3():
            put("sp", lambda e: e.dma_start(gint[:, :], A["int_g"].partition_broadcast(128)), ("c_gi", 0), r_free["cgi"], dma=True)
            put("sp", lambda e: e.dma_start(beint[:, :], A["int_be"].partition_broadcast(128)), ("c_be", 0), r_free["cbe"], dma=True)

        def split3(src, dst, tag, needs, room=None):
            a, b = room or (P["t1"], P["t2"])
            p1, p2 = b[:, 0:256].bitcast(BF16), b[:, 256:512].bitcast(BF16)
            k = lambda i: (f"s3_{i}", tag)
            put("act", lambda e: e.copy(p1, src), k(0), list(needs) + [("s3_5", tag - 1)])
            put("dve", lambda e: e.tensor_tensor(src, src, p1, ALU.subtract), k(1), [k(0), *needs])
            put("dve", lambda e: e.tensor_scalar(a[:, :], p1, cst[:, 1:2], None, ALU.mult), k(2), [k(0), ("c_cst", 0), ("s3_6", tag - 1)])
            put("act", lambda e: e.copy(p2, src), k(3), [k(1)])
            put("dve", lambda e: e.tensor_tensor(src, src, p2, ALU.subtract), k(4), [k(3)])
            put("dve", lambda e: e.scalar_tensor_tensor(out=a[:, :], in0=p2, scalar=cst[:, 2:3], in1=a[:, :], op0=ALU.mult, op1=ALU.add), k(5), [k(2), k(3)])
            put("dve", lambda e: e.scalar_tensor_tensor(out=dst, in0=src, scalar=cst[:, 3:4], in1=a[:, :], op0=ALU.mult, op1=ALU.add), k(6), [k(4), k(5)])

        def bias_table():
            split3(P["t0"][:, :], biasT[:, :], 0, [("c_rb", 0)])
            r_free["ct0"] = (("s3_6", 0),)

        def g_table(n):
            name, w = (("t", 1), ("s", 5), ("h", 0))[n]
            sl, c, key = load_chunk(A["rows_" + name], w_slots[0][2 + n % 2])
            put("dve", lambda e: e.tensor_scalar(c, c, w6[:, w:w + 1], None, ALU.mult), ("gw", n), [key, ("w6", 0)])
            split3(c, GT[name][:, :], 1 + n, [("gw", n)])
            r_free[sl] = (("s3_6", 1 + n),)

        def weights_softmax():
            aw = P["aw"]
            put("dve", lambda e: e.tensor_reduce(small[:, 1:2], aw[:, :], axis=AX.X, op=ALU.max), ("wm", 0), [("c_aw", 0)])
            put("dve", lambda e: e.tensor_scalar(aw[:, :], aw[:, :], small[:, 1:2], None, ALU.subtract), ("ws", 0), [("wm", 0)])
            put("act", lambda e: e.activation(aw[:, :], aw[:, :], ACT.Exp), ("we", 0), [("ws", 0)])
            put("dve", lambda e: e.tensor_reduce(small[:, 2:3], aw[:, :], axis=AX.X, op=ALU.add), ("wd", 0), [("we", 0)])
            put("dve", lambda e: e.reciprocal(small[:, 3:4], small[:, 2:3]), ("wr", 0), [("wd", 0)])
            put("dve", lambda e: e.tensor_scalar(w6[:, :], aw[:, :], small[:, 3:4], None, ALU.mult), ("w6", 0), [("wr", 0)])

        aff_slots = ((None, None), (("cSE", SE[:, :]), ("cET", ET[:, :])))
        more_slots = [("cgi", gint[:, :]), ("cbe", beint[:, :])]
        w_slots = ((("cr0", P["r0"][:, :]), ("cr1", P["r1"][:, :]), ("cxb2", xb[2][:, :]), ("cxb3", xb[3][:, :])),
                   (("pgb0", pgb[:, 0:512]), ("pgb1", pgb[:, 512:1024]), ("cz", z[:, :]), ("ct0", P["t0"][:, :])))

        def style(L):
            nm = "ko"[L]
            s, bank, free = xp_bank()
            cs = [load_chunk(A[nm + "_affT"][st], aff_slots[L][st]) for st in range(2)]
            for kt in range(4):
                for st in range(2):
                    put("pe", lambda e, kt=kt, st=st: mm(
                        e, bank[:, kt * 4:kt * 4 + 4], cs[st][1][:, kt * 128:kt * 128 + 128], P["condT"][:, st, :], start=(kt == 0 and st == 0)),
                        ("sty", L) if (kt == 3 and st == 1) else None, [cs[st][2], ("c_cond", 0), *free])
            for c in cs:
                r_free[c[0]] = (("sty", L),)
            put("dve", lambda e: e.tensor_tensor(
                styl[:, L, :, :], bank[:, 0:16].rearrange("p (k b) -> p k b", b=4),
                P["abc"][:, L, :].unsqueeze(2).to_broadcast([128, 4, 4]), ALU.add), ("styl", L), [("sty", L), ("c_abc", 0)])
            xp_free[s] = (("styl", L),)
            put("dve", lambda e: e.tensor_tensor(P["st2"][:, L, :, :], styl[:, L, :, :], styl[:, L, :, :], ALU.mult), ("stsq", L), [("styl", L)])

        def demodulation(L):
            nm = "ko"[L]
            cs = kept[L] = [load_chunk(A[nm + "_wT"][kt], w_slots[L][kt]) for kt in range(4)]
            s, bank, free = xp_bank()
            for kt in range(4):
                c = cs[kt]
                ys, y, yf = y_buf()
                put("act", lambda e, c=c, y=y: e.activation(y[:, :], c[1], ACT.Square), ("wsq", L * 4 + kt), [c[2], *yf])
                for ob in range(4):
                    put("pe", lambda e, y=y, kt=kt, ob=ob: mm(e, bank[:, ob * 4:ob * 4 + 4], y[:, ob * 128:ob * 128 + 128], P["st2"][:, L, kt, :], start=(kt == 0 and ob == 0)),
                        ("dmm", L * 4 + kt) if ob == 3 else None, [("wsq", L * 4 + kt), ("stsq", L), *free])
                y_free[ys] = (("dmm", L * 4 + kt),)
            dm_bank[L] = s, bank

        dm_bank = {}

        def demodulation2(L):
            s, bank = dm_bank[L]
            v = P["v"][:, L, :]
            put("dve", lambda e: e.tensor_scalar(v, bank[:, 0:16], 1e-8, None, ALU.add), ("dme", L), [("dmm", L * 4 + 3)])
            xp_free[s] = (("dme", L),)
            put("pool", lambda e: e.tensor_tensor(dmT[:, L, :], v, mh.to_broadcast([128, 16]), ALU.pow), ("dmp", L), [("dme", L), ("c_cst", 0)])

        kept = {}

        def mod_rows(b, L):
            n = b * 2 + L
            s, bank, free = xp_bank()
            for ob in range(4):
                put("pe", lambda e, ob=ob: mm(e, bank[:, ob * 128:ob * 128 + 128], dmT[:, L, ob * 4 + b:ob * 4 + b + 1].to_broadcast([128, 128]), ident[:, :], start=(ob == 0)),
                    ("dbc", n) if ob == 3 else None, [("dmp", L), ("c_id", 0), *free])
            put("act", lambda e: e.copy(dmb[:, :], bank[:, :]), ("dmb", n), [("dbc", n), ("stt", 4 * n - 1)])
            xp_free[s] = (("dmb", n),)

        def mod_load(b, L, kts):
            for kt in kts:
                mod_chunk[b, L, kt] = kept[L][kt] if b == 0 else load_chunk(A["ko"[L] + "_wT"][kt])

        mod_chunk = {}

        def mod_weights(b, L, kts):
            nm = "ko"[L]
            n = b * 2 + L
            last_use = ("A", 8 * b - 1) if L == 0 else ("O", 8 * b - 1)
            ys_ = {}
            for kt in [*kts, None]:
                if kt is not None:
                    c = mod_chunk[b, L, kt]
                    ys, y, yf = y_buf()
                    ys_[kt] = ys, y
                    put("dve", lambda e, c=c, y=y, kt=kt: e.scalar_tensor_tensor(
                        out=y[:, :], in0=c[1], scalar=styl[:, L, kt, b:b + 1], in1=dmb[:, :], op0=ALU.mult, op1=ALU.mult),
                        ("stt", 4 * n + kt), [c[2], ("dmb", n), ("styl", L), *yf])
                    r_free[c[0]] = (("stt", 4 * n + kt),)
                    put("act", lambda e, y=y, kt=kt: e.copy(WL[nm, "h"][:, kt, :], y[:, :]), ("mwh", 4 * n + kt), [("stt", 4 * n + kt), last_use])
                kp = kts[-1] if kt is None else kt - 1
                if kp >= kts[0]:
                    ys, y = ys_[kp]
                    put("dve", lambda e, y=y, kt=kp: e.tensor_tensor(WL[nm, "l"][:, kt, :], y[:, :], WL[nm, "h"][:, kt, :].bitcast(F32), ALU.subtract),
                        ("mwl", 4 * n + kp), [("mwh", 4 * n + kp), last_use])
                    y_free[ys] = (("mwl", 4 * n + kp),)
            mw_done[b, L] = [("mwh", 4 * n + 3), ("mwl", 4 * n + 3)]

        mw_done = {}
        nw = [0]

        def split_weight(y, ykeys, H, Lo, kt, eng):
            i = nw[0]
            nw[0] += 1
            put("act", lambda e: e.copy(H[:, kt, :], y), ("wh", i), ykeys)
            put(eng, lambda e: e.tensor_tensor(Lo[:, kt, :], y, H[:, kt, :].bitcast(F32), ALU.subtract), ("wl", i), [("wh", i)])
            return (("wh", i), ("wl", i))

        def w2_weights():
            for kt in range(4):
                cs, c, key = load_chunk(A["int_w2"][kt])
                rd = split_weight(c, [key], WL["2", "h"], WL["2", "l"], kt, ("pool", "dve")[kt % 2])
                r_free[cs] = rd
                w2_done[0] = [*w2_done[0], *rd]
                yield

        w2_done = [()]

        nets = [("mem", 0, (0, 1)), ("noi", 32, (2,)), ("res", 64, (3,))]

        def zeros(bank, i, needs):
            z0 = P["L2"][:, :, :].rearrange("p a b -> p (a b)")
            put("pe", lambda e: mm(e, bank[:, 0:384], z0[:, 0:128], z0, start=True), None, needs)
            put("pe", lambda e: mm(e, bank[:, 384:512], z0[:, 0:128], z0[:, 0:128]), ("mz", i))

        def mlp1():
            h, hT = P["h"], P["hT"]
            bank = ps["acc1"]
            zeros(bank, 0, [("c_z", 0)])
            for i, (n, r, cs_) in enumerate(nets):
                for j, ci in enumerate(cs_):
                    sl, c, key = load_chunk(A[n + "_w1"][j])
                    put("pe", lambda e, r=r, ci=ci, c=c: mm(e, bank[r:r + 4, :], P["condT"][:, ci, :], c), ("m1", i * 2 + j), [key])
                    r_free[sl] = (("m1", i * 2 + j),)
                    yield
            cv = load_chunk(A["rows_v"][0])
            put("dve", lambda e: e.tensor_tensor(h[:, :], bank[:, :], cv[1], ALU.add), ("mh", 0), [("m1", 4), cv[2]])
            r_free[cv[0]] = (("mh", 0),)
            put("act", lambda e: e.activation(h[:, :], h[:, :], ACT.Silu), ("mh2", 0), [("mh", 0)])
            yield
            s, bank2, free = xp_bank()
            for kt in range(4):
                put("pe", lambda e, kt=kt: e.transpose(bank2[:, kt * 128:kt * 128 + 128], h[:, kt * 128:kt * 128 + 128], ident[:, :]),
                    ("mt", kt), [("mh2", 0), ("c_id", 0), *free])
            put("act", lambda e: e.copy(hT[:, :, :].rearrange("p a b -> p (a b)"), bank2[:, :]), ("mhT", 0), [("mt", 3)])
            xp_free[s] = (("mhT", 0),)
            yield

        def mlp2():
            h, hT = P["h"], P["hT"]
            bank = ps["acc1"]
            zeros(bank, 1, [("mh", 0)])
            for i, (n, r, _) in enumerate(nets):
                for kt in range(4):
                    sl, c, key = load_chunk(A[n + "_w2"][kt])
                    put("pe", lambda e, r=r, kt=kt, c=c: mm(e, bank[r:r + 4, :], hT[:, kt, r:r + 4], c),
                        ("m2", i * 4 + kt), [key, ("mhT", 0)])
                    r_free[sl] = (("m2", i * 4 + kt),)
                    yield
            cv = [load_chunk(A["rows_v"][j]) for j in (1, 2, 3)]
            put("dve", lambda e: e.tensor_tensor(h[:, :], bank[:, :], cv[0][1], ALU.add), ("mv0", 0), [("m2", 11), cv[0][2], ("mt", 3)])
            r_free[cv[0][0]] = (("mv0", 0),)
            table_rows(5, 2, [("mz", 1)])
            bs = small[:, 8:14]
            mv = small[:, 14:16]
            put("dve", lambda e: e.bn_stats(bs, h[:, :]), ("mv1", 0), [("mv0", 0)])
            put("dve", lambda e: e.bn_aggr(mv, bs), ("mv2", 0), [("mv1", 0)])
            put("pool", lambda e: e.tensor_tensor(small[:, 16:17], mv[:, 1:2], eps5, ALU.add), ("mv3", 0), [("mv2", 0), ("c_eps", 0)])
            put("pool", lambda e: e.tensor_tensor(small[:, 17:18], small[:, 16:17], mh, ALU.pow), ("mv4", 0), [("mv3", 0), ("c_cst", 0)])
            put("dve", lambda e: e.tensor_scalar(h[:, :], h[:, :], mv[:, 0:1], small[:, 17:18], ALU.subtract, ALU.mult), ("mv5", 0), [("mv4", 0)])
            put("dve", lambda e: e.tensor_tensor(h[:, :], h[:, :], cv[1][1], ALU.mult), ("mv6", 0), [("mv5", 0), cv[1][2]])
            r_free[cv[1][0]] = (("mv6", 0),)
            put("dve", lambda e: e.tensor_tensor(h[:, :], h[:, :], cv[2][1], ALU.add), ("mv7", 0), [("mv6", 0), cv[2][2]])
            r_free[cv[2][0]] = (("mv7", 0),)
            yield

        def mlp3():
            h, hT = P["h"], P["hT"]
            s, bank2, free = xp_bank()
            for kt in range(4):
                put("pe", lambda e, kt=kt: e.transpose(bank2[:, kt * 128:kt * 128 + 128], h[:, kt * 128:kt * 128 + 128], ident[:, :]),
                    ("mu", kt), [("mv7", 0), *free])
            put("act", lambda e: e.copy(hT[:, :, :].rearrange("p a b -> p (a b)"), bank2[:, :]), ("vT", 0), [("mu", 3), ("m2", 11)])
            xp_free[s] = (("vT", 0),)
            yield

        spec = [("m", 2, "hT", 0, 4, 64), ("n", 3, "hT", 32, 4, 64), ("r", 4, "hT", 64, 4, 64),
                ("t", 1, "tabT", 32, 5, 0), ("s", 5, "tabT", 64, 3, 32), ("h", 0, "tabT", 0, 5, 0)]
        block_of = {"h": 0, "t": 1, "m": 2, "n": 3, "r": 4, "s": 5}
        Pp = ps["acc0"]

        def LB(slot):
            if slot < 3:
                return P[f"L{slot}"][:, :, :]
            return (xb[2], xb[3], dmb)[slot - 3][:, 0:384].rearrange("p (a b) -> p a b", b=96)

        def table_rows(j, slot, free):
            name, w, src, c0, n, base = spec[j]
            t = LB(slot)
            put("pool", lambda e: e.memset(t, 0.0), ("lz", j), free)
            for rep in range(3):
                put("dve", lambda e, rep=rep: e.tensor_scalar(t[:, :, base + 8 * rep:base + n + 8 * rep], P[src][:, :, c0:c0 + n], w6[:, w:w + 1], None, ALU.mult),
                    ("lb", 3 * j + rep), [("lz", j), ("w6", 0), ("vT", 0) if src == "hT" else ("c_tabT", 0)])

        def w1_ths(j, start=False):
            name = spec[j][0]
            t = LB(j - 3)
            for kt in range(4):
                sl, c, key = load_chunk(A["int_w1"][block_of[name] * 4 + kt])
                put("pe", lambda e, kt=kt, c=c: mm(e, Pp[0:96, :], t[:, kt, :], c, start=(start and kt == 0)), ("Pm", (j - 3) * 4 + kt), [key, ("lb", 3 * j + 2)])
                rd = split_weight(c, [key], W1[name, "h"], W1[name, "l"], kt, ("pool", "dve")[kt % 2])
                r_free[sl] = (("Pm", (j - 3) * 4 + kt), *rd)
                w1_done[name] = [*w1_done.get(name, ()), *rd]
                yield

        def w1_x():
            Ls = [LB(j + 3) for j in range(3)]
            for kt in range(4):
                xacc = (P["h"], P["t1"])[kt % 2]
                for j in range(3):
                    name, w = spec[j][:2]
                    sl, c, key = load_chunk(A["int_w1"][block_of[name] * 4 + kt])
                    i = 12 + kt * 3 + j
                    put("pe", lambda e, j=j, kt=kt, c=c: mm(e, Pp[0:96, :], Ls[j][:, kt, :], c), ("Pm", i), [key, ("lb", 3 * j + 2)])
                    if j == 0:
                        put("dve", lambda e, c=c, w=w, xacc=xacc: e.tensor_scalar(xacc[:, :], c, w6[:, w:w + 1], None, ALU.mult), ("xa", 3 * kt), [key, ("mu", 3), ("s3_6", 3), *xfree[kt % 2]])
                    else:
                        put("dve", lambda e, c=c, w=w, xacc=xacc: e.scalar_tensor_tensor(out=xacc[:, :], in0=c, scalar=w6[:, w:w + 1], in1=xacc[:, :], op0=ALU.mult, op1=ALU.add),
                            ("xa", 3 * kt + j), [key, ("xa", 3 * kt + j - 1)])
                    r_free[sl] = (("Pm", i), ("xa", 3 * kt + j))
                    yield
                xfree[kt % 2] = split_weight(xacc[:, :], [("xa", 3 * kt + 2)], W1["x", "h"], W1["x", "l"], kt, "pool")
                w1_done["x"] = [*w1_done.get("x", ()), *xfree[kt % 2]]

        def table_P():
            t0 = P["t0"]
            put("sp", lambda e: e.dma_start(t0[:, :], A["rows_p"]), ("pb", 0), [("stt", 7)], dma=True)
            put("dve", lambda e: e.tensor_copy(xb[2][96:128, :], t0[96:128, :]), None, [("pb", 0), ("Pm", 23)])
            put("dve", lambda e: e.tensor_tensor(xb[2][0:96, :], t0[0:96, :], Pp[0:96, :], ALU.add), ("pbs", 0), [("pb", 0), ("Pm", 23)])

        def table_P2():
            split3(xb[2][:, :], PT[:, :], 4, [("pbs", 0)], (xb[3], dmb))

        xfree = [(), ()]
        w1_done = {}

        def load_x(g):
            put("sp", lambda e: e.dma_start(xraw[:, :, :], A["xT"][g]), ("ldx", g), [("xlo", g - 1), ("xhi", g - 1)], dma=True)

        def load_tok(g):
            s = g % 4
            put("sp", lambda e: e.dma_start(xb[s][:, :], A["x"][g * 128:g * 128 + 128, :]), (f"ldt{s}", g), [(f"out{s}", g - 4), *([("s3_6", 4)] if g in (2, 3) else [])], dma=True)

        def split_x(g):
            put("act", lambda e: e.copy(xhi[:, :, :], xraw[:, :, :]), ("xhi", g), [("ldx", g), ("A", g - 1)])
            put("pool", lambda e: e.tensor_tensor(xlo[:, :, :], xraw[:, :, :], xhi[:, :, :].bitcast(F32), ALU.subtract), ("xlo", g), [("xhi", g), ("ldx", g), ("A", g - 1)])

        qslot = {}

        def stage_A(g):
            s, bank, free = tok_bank()
            b = g // 8
            for kt in range(4):
                put("pe", lambda e, kt=kt: three(e, bank[:, :], xhi[:, kt, :], xlo[:, kt, :], WL["k", "h"][:, kt, :], WL["k", "l"][:, kt, :], kt == 0),
                    None, [("xhi", g), ("xlo", g), *mw_done[b, 0], *free])
            put("pe", lambda e: mm(e, bank[:, :], selT[:, 0, :], biasT[:, :]), ("A", g), [("c_sel", 0), ("s3_6", 0)])
            put("dve", lambda e: e.transpose(q[:, :].rearrange("p (t h) -> p h t", h=16), bank[:, :].rearrange("p (h t) -> p h t", h=16)),
                ("qT", g), [("A", g), ("q3", g - 1), ("q2", g - 1)])
            tok_free[s] = (("qT", g),)

        def stage_A1(g):
            put("act", lambda e: e.copy(q12[:, :, 0], q[:, :]), ("q1", g), [("qT", g), *q12_used(g)])
            put("pool", lambda e: e.tensor_tensor(q[:, :], q[:, :], q12[:, :, 0], ALU.subtract), ("qr", g), [("q1", g), ("qT", g)])

        def q12_used(g):
            return [("S", 2 * g - 1), ("VT", g - 1), ("bdq", g - 1)]

        def stage_A2(g):
            put("act", lambda e: e.copy(q12[:, :, 1], q[:, :]), ("q2", g), [("qr", g), *q12_used(g)])
            put("pool", lambda e: e.tensor_tensor(q3[:, :], q[:, :], q12[:, :, 1], ALU.subtract), ("q3", g), [("q2", g), ("S", 2 * g - 1), ("VT3", g - 1), ("bdq3", g - 1)])

        def stage_bdq(g):
            for i in range(4):
                r = slice(32 * i, 32 * i + 32)
                put("dve", lambda e, i=i, r=r: e.tensor_copy(BD12[r, :, i, :, :].rearrange("p g m t -> p g (m t)"), q12[r, :, :].rearrange("p (g m) t -> p g (m t)", g=16)),
                    ("bdq", g) if i == 3 else None, [("q1", g), ("q2", g), ("AV", 2 * g - 1), ("c_bd12", 0)])
            for i in range(4):
                r = slice(32 * i, 32 * i + 32)
                put("act", lambda e, i=i, r=r: e.copy(BD3[r, :, i, :], q3[r, :].rearrange("p (g m) -> p g m", g=16)),
                    ("bdq3", g) if i == 3 else None, [("q3", g), ("S", 2 * g - 1), ("c_bd3", 0)])

        def stage_V(g):
            put("dve", lambda e: e.transpose(v12[:, :, :].rearrange("p a b -> p (a b)").bitcast(U32), q12[:, :, :].rearrange("p a b -> p (a b)").bitcast(U32)),
                ("VT", g), [("q1", g), ("q2", g), ("AV", 2 * g - 1)])
            put("dve", lambda e: e.transpose(v3[:, :], q3[:, :]), ("VT3", g), [("q3", g), ("AV", 2 * g - 1)])

        mx, den, rden = small[:, 18:34], small[:, 34:50], small[:, 50:66]

        def by_head(t):
            return t[:, :].rearrange("p (g m) -> p g m", m=32)

        def att_half(h, t):
            return att[:, h * 512:h * 512 + 512].rearrange("p (c t) -> p c t", t=2)[:, :, t]

        def add_parts(g, stage, free):
            for h in range(2):
                c = SE[:, h * 256:h * 256 + 256]
                put("act", lambda e, h=h, c=c: e.copy(c, att_half(h, 1)), (stage + "c", 2 * g + h), [(stage, 2 * g + h), *free])
                put("dve", lambda e, h=h, c=c: e.tensor_tensor(c, att_half(h, 0), c, ALU.add), (stage + "s", 2 * g + h), [(stage + "c", 2 * g + h), *free])

        def stage_S(g):
            def run(e, j):
                c = slice(j * 32, j * 32 + 32)
                both = att[:, j * 64:j * 64 + 64]
                one = both.rearrange("p (m t) -> p m t", t=2)[:, :, 0]
                w1 = BD12[:, j, :, :, 0].rearrange("p a b -> p (a b)")
                w2 = BD12[:, j, :, :, 1].rearrange("p a b -> p (a b)")
                w3 = BD3[:, j, :, :].rearrange("p a b -> p (a b)")
                r12 = q12[:, c, :].rearrange("p m t -> p (m t)")
                mm(e, both, w1, r12)
                mm(e, one, w1, q3[:, c])
                mm(e, both, w2, r12)
                return mm(e, one, w3, q12[:, c, 0])

            for h in range(2):
                v = att_half(h, 0).rearrange("p (g m) -> p g m", m=32)
                put("pe", lambda e, v=v: mm(e, v, maskL[:, :], maskR[:, :].unsqueeze(1).to_broadcast([128, 8, 32]), start=True), None,
                    [("AVs", 2 * g - 1), ("c_mL", 0), ("c_mR", 0)])
            for j in range(16):
                put("pe", lambda e, j=j: run(e, j), ("S", 2 * g + j // 8) if j % 8 == 7 else None, [("bdq", g), ("bdq3", g), ("q3", g)])

        def stage_S1(g):
            v = by_head
            add_parts(g, "S", [("aTr", g - 1), ("sty", 1)])

        def stage_max(g):
            v = by_head
            put("dve", lambda e: e.tensor_reduce(mx, v(SE), axis=AX.X, op=ALU.max), ("mx", g), [("Ss", 2 * g + 1), ("sub", g - 1)])
            put("dve", lambda e: e.tensor_tensor(v(SE), v(SE), mx.unsqueeze(2).to_broadcast([128, 16, 32]), ALU.subtract),
                ("sub", g), [("mx", g)])
            put("act", lambda e: e.activation(SE[:, :], SE[:, :], ACT.Exp, scale=SCALE), ("exp", g), [("sub", g)])

        def stage_E(g, between=None):
            v = by_head
            put("dve", lambda e: e.transpose(ET[:, :], SE[:, :]), ("ET", g), [("exp", g), ("nT2", g - 1), ("sty", 1)])
            put("act", lambda e: e.copy(e12[:, :, 0], ET[:, :]), ("e1", g), [("ET", g), ("bde", g - 1)])
            put("dve", lambda e: e.tensor_reduce(den, v(SE), axis=AX.X, op=ALU.add), ("den", g), [("exp", g)])
            if between is not None:
                between()
            put("dve", lambda e: e.tensor_tensor(e12[:, :, 1], ET[:, :], e12[:, :, 0], ALU.subtract), ("e2", g), [("e1", g), ("ET", g), ("bde", g - 1)])
            put("dve", lambda e: e.reciprocal(rden, den), ("rden", g), [("den", g), ("norm", g - 1)])
            for i in range(4):
                r = slice(32 * i, 32 * i + 32)
                put("dve", lambda e, i=i, r=r: e.tensor_copy(BD12[r, :, i, :, :].rearrange("p g m t -> p g (m t)").bitcast(F16), e12[r, :, :].rearrange("p (g m) t -> p g (m t)", g=16)),
                    ("bde", g) if i == 3 else None, [("e1", g), ("e2", g), ("S", 2 * g + 1)])

        def stage_AV(g):
            def run(e, j):
                c = slice(j * 32, j * 32 + 32)
                both = att[:, j * 64:j * 64 + 64]
                one = both.rearrange("p (m t) -> p m t", t=2)[:, :, 0]
                w1 = BD12[:, j, :, :, 0].rearrange("p a b -> p (a b)").bitcast(F16)
                w2 = BD12[:, j, :, :, 1].rearrange("p a b -> p (a b)").bitcast(F16)
                v12_ = v12[:, c, :].rearrange("p m t -> p (m t)")
                mm(e, both, w1, v12_, start=(j % 8 == 0))
                mm(e, one, w1, v3[:, c])
                return mm(e, both, w2, v12_)

            for j in range(16):
                put("pe", lambda e, j=j: run(e, j), ("AV", 2 * g + j // 8) if j % 8 == 7 else None, [("bde", g), ("VT", g), ("VT3", g), ("Ss", 2 * g + 1)])
            v = by_head
            add_parts(g, "AV", [("den", g), ("ET", g)])
            put("dve", lambda e: e.tensor_tensor(v(SE), v(SE), rden.unsqueeze(2).to_broadcast([128, 16, 32]), ALU.mult), ("norm", g), [("AVs", 2 * g + 1), ("rden", g)])

        def stage_nT(g):
            put("dve", lambda e: e.transpose(ET[:, :].rearrange("p (h g t) -> p g t h", h=16, t=2), SE[:, :]), ("nT", g), [("norm", g), ("e1", g), ("e2", g)])
            put("dve", lambda e: e.transpose(SE[:, :], ET[:, :]), ("nT2", g), [("nT", g)])

        def stage_aTr(g):
            s, bank, free = xp_bank()
            for c in range(4):
                put("pe", lambda e, c=c: e.transpose(bank[:, c * 128:c * 128 + 128], SE[:, c * 128:c * 128 + 128], ident[:, :]),
                    ("aTr", g) if c == 3 else None, [("nT2", g), ("c_id", 0), *free])
            v = bank[:, :].rearrange("p (c t) -> p c t", c=4)
            put("act", lambda e: e.copy(ahi[:, :, :], v), ("ahi", g), [("aTr", g), ("O", g - 1)])
            av_bank[g] = s, v

        av_bank = {}

        def stage_alo(g):
            s, v = av_bank[g]
            put("dve", lambda e: e.tensor_tensor(alo[:, :, :], v, ahi[:, :, :].bitcast(F32), ALU.subtract), ("alo", g), [("ahi", g), ("O", g - 1)])
            xp_free[s] = (("alo", g),)

        st1, mv1, rs1 = small[:, 66:72], small[:, 72:74], small[:, 74:76]
        st2_, mv2, rs2 = small[:, 76:82], small[:, 82:84], small[:, 84:86]
        st3, mv3, rs3 = small[:, 86:92], small[:, 92:94], small[:, 94:96]

        def stage_O(g):
            s, bank, free = tok_bank()
            b = g // 8
            xs = xb[g % 4]
            for kt in range(4):
                put("pe", lambda e, kt=kt: three(e, bank[:, :], ahi[:, kt, :], alo[:, kt, :], WL["o", "h"][:, kt, :], WL["o", "l"][:, kt, :], kt == 0),
                    None, [("ahi", g), ("alo", g), *mw_done[b, 1], *free])
            put("pe", lambda e: mm(e, bank[:, :], selT[:, 1, :], biasT[:, :]), ("O", g), [])
            put("dve", lambda e: e.tensor_tensor(xs[:, :], bank[:, :], xs[:, :], ALU.add), ("x1", g), [("O", g), (f"ldt{g % 4}", g)])
            tok_free[s] = (("x1", g),)
            put("dve", lambda e: e.bn_stats(st1, xs[:, :]), ("b1", g), [("x1", g)])
            put("dve", lambda e: e.bn_aggr(mv1, st1), ("a1", g), [("b1", g), ("z", g - 1)])
            put("pool", lambda e: e.tensor_tensor(rs1[:, 0:1], mv1[:, 1:2], eps5, ALU.add), ("r1a", g), [("a1", g), ("c_eps", 0), ("r1", g - 1)])
            put("pool", lambda e: e.tensor_tensor(rs1[:, 1:2], rs1[:, 0:1], mh, ALU.pow), ("r1", g), [("r1a", g), ("z", g - 1), ("c_cst", 0)])

        def stage_z(g):
            xs = xb[g % 4]
            put("dve", lambda e: e.tensor_scalar(z[:, :], xs[:, :], mv1[:, 0:1], rs1[:, 1:2], ALU.subtract, ALU.mult), ("z", g), [("r1", g), ("zTr", g - 1), ("v1", g - 1), ("stt", 6)])

        def stage_v(g):
            pg, pb = pgb[:, 0:512], pgb[:, 512:1024]
            put("pool", lambda e: e.tensor_tensor(pg, z[:, :], pg, ALU.mult), ("v1", g), [("z", g), ("gat", g)])
            put("pool", lambda e: e.tensor_tensor(pg, pg, pb, ALU.add), ("v2", g), [("v1", g)])

        def stage_v2(g):
            pg = pgb[:, 0:512]
            put("dve", lambda e: e.bn_stats(st2_, pg), ("b2", g), [("v2", g)])
            put("dve", lambda e: e.bn_aggr(mv2, st2_), ("a2", g), [("b2", g), ("u", g - 1)])
            put("pool", lambda e: e.tensor_tensor(rs2[:, 0:1], mv2[:, 1:2], eps5, ALU.add), ("r2a", g), [("a2", g), ("r2", g - 1)])
            put("pool", lambda e: e.tensor_tensor(rs2[:, 1:2], rs2[:, 0:1], mh, ALU.pow), ("r2", g), [("r2a", g), ("u", g - 1)])

        def stage_u(g):
            pg = pgb[:, 0:512]
            put("dve", lambda e: e.tensor_scalar(pg, pg, mv2[:, 0:1], rs2[:, 1:2], ALU.subtract, ALU.mult), ("u", g), [("r2", g), ("v2", g)])

        def gather(g):
            off = bass.IndirectOffsetOnAxis(ap=pidx[:, g:g + 1].bitcast(U32), axis=0)
            put("pool", lambda e: e.indirect_dma_start(pgb[:, :], None, A["pw"], off), ("gat", g), [("uTr", g - 1), ("v2", g - 1), ("c_pidx", 0), ("stt", 5)], dma=True)

        def xpose(g, src, needs, key):
            s, bank, free = xp_bank()
            for c in range(4):
                put("pe", lambda e, c=c: e.transpose(bank[:, c * 128:c * 128 + 128], src[:, c * 128:c * 128 + 128], ident[:, :]),
                    key if c == 3 else None, [*needs, ("c_id", 0), *free])
            return s, bank[:, :].rearrange("p (c t) -> p c t", c=4)

        def half(g):
            return slice((g % 2) * 128, (g % 2) * 128 + 128)

        def stage_x1T(g):
            k = g // 2
            s, v = xpose(g, xb[g % 4], [("x1", g)], ("xTr", g))
            h = half(g)
            put("act", lambda e: e.copy(op[0]["h"][:, :, h], v), ("oxh", g), [("xTr", g), ("W2", 2 * k - 1), *pro_end])
            xt[g] = s, v, h

        xt = {}

        def stage_x1T2(g):
            s, v, h = xt[g]
            k = g // 2
            put("dve", lambda e: e.tensor_tensor(op[0]["l"][:, :, h], v, op[0]["h"][:, :, h].bitcast(F32), ALU.subtract), ("oxl", g), [("oxh", g), ("W2", 2 * k - 1)])
            xp_free[s] = (("oxl", g),)

        def stage_xbe(g):
            put("pool", lambda e: e.tensor_tensor(xb[g % 4][:, :], xb[g % 4][:, :], beint[:, :], ALU.add), ("xbe", g), [("xTr", g), ("z", g), ("b1", g), ("c_be", 0)])

        def stage_zT(g):
            s, v = xpose(g, z, [("z", g)], ("zTr", g))
            put("act", lambda e: e.copy(zT[:, :, half(g)], v), ("zT", g), [("zTr", g), ("prod_s", g - 2), ("prod_t", g - 2), *pro_end])
            xp_free[s] = (("zT", g),)

        def stage_uT(g):
            s, v = xpose(g, pgb, [("u", g)], ("uTr", g))
            put("act", lambda e: e.copy(uT[:, :, :], v), ("uT", g), [("uTr", g), ("prod_h", g - 1), *pro_end])
            xp_free[s] = (("uT", g),)

        def one_hot(k):
            rd = [("oh", k - 1)]
            t = slice(k * 256, k * 256 + 256)
            for i, nm in enumerate(("cid", "sid", "bid")):
                put("sp", lambda e, i=i, nm=nm: e.dma_start(ids[32 * i:32 * i + 32, :], A[nm][t].partition_broadcast(32)),
                    ("ids", k * 3 + i), [*rd, ("c_ids", 0)], dma=True)

        def one_hot2(k):
            s = k % 2
            used = [("W1x1", k - 2), ("Gs", 2 * k - 3), ("Gh", 2 * k - 3)]
            put("dve", lambda e: e.tensor_scalar(OH[s][:, :], ids[:, :], cst[:, 0:1], None, ALU.is_equal), ("oh", k), [("ids", k * 3 + 2), ("c_cst", 0), *used])

        def product(g, name):
            k = g // 2
            s, bank, free = xp_bank()
            tab = GT[name]
            nG = {"t": 0, "s": 1, "h": 2}[name]
            for c in range(4):
                put("pe", lambda e, c=c: mm(e, bank[:, c * 128:c * 128 + 128], tab[:, c * 128:c * 128 + 128], OH[k % 2][:, half(g)], start=(c == 0)),
                    ("G" + name, g) if c == 3 else None, [("oh", k), ("s3_6", 1 + nG), *free])
            pr[name, g] = s, bank

        pr = {}

        def product2(g, name, src, srckey, slot, freekeys):
            s, bank = pr[name, g]
            ys, y, yf = y_buf()
            yv = y[:, :].rearrange("p (c t) -> p c t", c=4)
            put("dve", lambda e: e.tensor_tensor(yv, src, bank[:, :].rearrange("p (c t) -> p c t", c=4), ALU.mult), ("prod_" + name, g), [("G" + name, g), srckey, *yf])
            xp_free[s] = (("prod_" + name, g),)
            h = half(g)
            put("act", lambda e: e.copy(op[slot]["h"][:, :, h], yv), (f"o{name}h", g), [("prod_" + name, g), *freekeys])
            put("pool", lambda e: e.tensor_tensor(op[slot]["l"][:, :, h], yv, op[slot]["h"][:, :, h].bitcast(F32), ALU.subtract), (f"o{name}l", g), [(f"o{name}h", g), *freekeys])
            y_free[ys] = ((f"o{name}l", g),)

        def stage_t(g):
            product2(g, "t", zT[:, :, half(g)], ("zT", g), 1, [("W1h1", g // 2 - 1)])

        def stage_s(g):
            product2(g, "s", zT[:, :, half(g)], ("zT", g), 0, [("W1x1", g // 2)])

        def stage_h(g):
            product2(g, "h", uT[:, :, :], ("uT", g), 1, [("W1t1", g // 2)])

        slot_of = {"x": 0, "t": 1, "s": 0, "h": 1}

        def stage_W1(k, name, pair, js=(0, 1)):
            acc = ps[f"acc{pair}"]
            o = op[slot_of[name]]
            needs = [(f"o{name}h", 2 * k + 1), (f"o{name}l", 2 * k + 1), *w1_done[name]]
            for j in js:
                m = 2 * pair + j
                dst = acc[:, j * 256:j * 256 + 256]
                ms = slice(m * 128, m * 128 + 128)
                if name == "x":
                    put("pe", lambda e, j=j, dst=dst, ms=ms: mm(e, dst, PT[:, ms], OH[k % 2][:, :], start=(j == 0)), None,
                        [("sil", 2 * (k - 1) + pair), ("oh", k), ("s3_6", 4), ("mv0", 0)])
                for kt in range(4):
                    put("pe", lambda e, kt=kt, dst=dst, ms=ms: three(e, dst, W1[name, "h"][:, kt, ms], W1[name, "l"][:, kt, ms], o["h"][:, kt, :], o["l"][:, kt, :], False),
                        (f"W1{name}{pair}", k) if (j == 1 and kt == 3) else None, needs)

        def stage_silu(k, pair):
            ys, y, yf = y_buf()
            n = 2 * k + pair
            acc = ps[f"acc{pair}"]
            c = slice(2 * pair, 2 * pair + 2)
            put("act", lambda e: e.activation(y[:, :], acc[:, :], ACT.Silu), ("sil", n), [(f"W1h{pair}", k), *yf])
            hv = lambda p: op[0][p][:, c, :].rearrange("p a b -> p (a b)")
            put("act", lambda e: e.copy(hv("h"), y[:, :]), ("ash", n), [("sil", n), ("W1s1", k)])
            sil[n] = ys, y, hv

        sil = {}

        def stage_silu2(k, pair):
            n = 2 * k + pair
            ys, y, hv = sil[n]
            put("dve", lambda e: e.tensor_tensor(hv("l"), y[:, :], hv("h").bitcast(F32), ALU.subtract), ("asl", n), [("ash", n), ("W1s1", k)])
            y_free[ys] = (("asl", n),)

        def stage_W2a(g):
            w2_bank[g] = tok_bank()
            W2_part(g, (0, 1))

        w2_bank = {}

        def W2_part(g, ms):
            k = g // 2
            s, bank, free = w2_bank[g]
            for m in ms:
                put("pe", lambda e, m=m: three(e, bank[:, :], op[0]["h"][:, m, half(g)], op[0]["l"][:, m, half(g)], WL["2", "h"][:, m, :], WL["2", "l"][:, m, :], m == 0),
                    None, [("ash", 2 * k + ms[0] // 2), ("asl", 2 * k + ms[0] // 2), *w2_done[0], *free])

        def stage_W2b(g):
            s, bank, free = w2_bank[g]
            W2_part(g, (2, 3))
            put("pe", lambda e: mm(e, bank[:, :], selT[:, 2, :], biasT[:, :]), ("W2", g), [])
            put("dve", lambda e: e.bn_stats(st3, bank[:, :]), ("b3", g), [("W2", g)])
            put("dve", lambda e: e.bn_aggr(mv3, st3), ("a3", g), [("b3", g), ("w", g - 1)])
            put("pool", lambda e: e.tensor_tensor(rs3[:, 0:1], mv3[:, 1:2], eps5, ALU.add), ("r3a", g), [("a3", g), ("r3", g - 1)])
            put("pool", lambda e: e.tensor_tensor(rs3[:, 1:2], rs3[:, 0:1], mh, ALU.pow), ("r3", g), [("r3a", g), ("fin", g - 1)])
            ys, y, yf = y_buf()
            put("dve", lambda e: e.scalar_tensor_tensor(out=y[:, :], in0=bank[:, :], scalar=mv3[:, 0:1], in1=gint[:, :], op0=ALU.subtract, op1=ALU.mult),
                ("w", g), [("a3", g), ("c_gi", 0), *yf])
            tok_free[s] = (("w", g),)
            w_tile[g] = ys, y

        w_tile = {}

        def stage_out(g):
            xs = xb[g % 4]
            ys, y = w_tile[g]
            put("dve", lambda e: e.scalar_tensor_tensor(out=xs[:, :], in0=y[:, :], scalar=rs3[:, 1:2], in1=xs[:, :], op0=ALU.mult, op1=ALU.add),
                ("fin", g), [("w", g), ("r3", g), ("xbe", g)])
            y_free[ys] = (("fin", g),)
            put("sp", lambda e: e.dma_start(out[g * 128:g * 128 + 128, :], xs[:, :]), (f"out{g % 4}", g), [("fin", g)], dma=True)

        pro_end = []

        def tables():
            yield from mlp1()
            table_rows(3, 0, [])
            table_rows(4, 1, [])
            yield from mlp2()
            yield from w1_ths(3, start=True)
            yield from mlp3()
            yield from w1_ths(4)
            g_table(2)
            for j in range(3):
                table_rows(j, 3 + j, [("s3_6", 3), ("stt", 7)])
            yield from w1_ths(5)
            yield from w1_x()
            yield from w2_weights()
            yield table_P()

        work = tables()

        def steps(n):
            for _ in range(n):
                next(work, None)

        def last_out(g):
            stage_out(g)
            for n in (g + 3, g + 4):
                if n < NG:
                    load_tok(n)

        all_kt = range(4)
        consts()
        style(0)
        demodulation(0)
        demodulation2(0)
        load_x(0)
        consts2()
        split_x(0)
        bias_table()
        mod_rows(0, 0)
        mod_load(0, 0, all_kt)
        mod_weights(0, 0, all_kt)
        one_hot(0)
        one_hot2(0)
        slots[:] = [*more_slots, *slots, *w_slots[0][0:2]]
        steps(5)
        weights_softmax()
        stage_A(0)
        steps(1)
        style(1)
        stage_A1(0)
        stage_A2(0)
        demodulation(1)
        load_x(1)
        one_hot(1)
        for g in range(2):
            load_tok(g)
        g_table(0)
        stage_bdq(0)
        stage_V(0)
        split_x(1)

        for k in range(NT + 1):
            a, b = 2 * k, 2 * k + 1
            pa, pb = a - 2, a - 1
            front, back, more = k < NT, k > 0, k < NT - 1
            next_mod = more and (a + 2) % 8 == 0
            this_mod = front and k and a % 8 == 0
            mod = ((a + 2) // 8, 0) if next_mod else (a // 8, 1) if this_mod else None
            if front:
                if next_mod:
                    mod_load(*mod, (0, 1))
                stage_S(a)
                if back:
                    stage_z(pb)
                    stage_x1T(pb)
                stage_S1(a)
                if back:
                    stage_x1T2(pb)
                    stage_xbe(pb)
                    stage_v(pb)
                stage_max(a)
                stage_A(b)
                stage_A1(b)
                if back:
                    stage_zT(pb)
                    product(pb, "t")
                if not back:
                    demodulation2(1)
                stage_E(a, (lambda: stage_t(pb)) if back else None)
                stage_A2(b)
                if k > 1:
                    last_out(pb - 2)
                if more:
                    load_x(a + 2)
            else:
                stage_x1T(pb)
                stage_x1T2(pb)
                stage_z(pb)
                stage_xbe(pb)
                stage_v(pb)
                last_out(pb - 2)
            if back:
                stage_W1(k - 1, "x", 0)
                if not front:
                    stage_zT(pb)
                    product(pb, "t")
                    stage_t(pb)
                if mod:
                    mod_rows(*mod)
                stage_v2(pb)
                if mod:
                    mod_weights(*mod, (0, 1))
                    mod_load(*mod, (2, 3))
                stage_W1(k - 1, "x", 1)
                product(pa, "s")
                if not front:
                    stage_u(pb)
                    stage_s(pa)
            else:
                g_table(1)
                steps(6)
            if front:
                stage_AV(a)
                if back:
                    stage_s(pa)
                stage_nT(a)
                if this_mod:
                    mod_weights(*mod, (2, 3))
                if back:
                    stage_u(pb)
                else:
                    mod_rows(0, 1)
                    mod_load(0, 1, all_kt)
                    mod_weights(0, 1, all_kt)
            if back:
                if not front:
                    product(pb, "s")
                    stage_s(pb)
                stage_W1(k - 1, "t", 0)
            if not back:
                steps(5)
            else:
                stage_W1(k - 1, "t", 1, (0,))
            if front:
                stage_aTr(a)
                if back:
                    product(pb, "s")
                if more:
                    split_x(a + 2)
                    if k:
                        load_x(b + 2)
                stage_alo(a)
                if back:
                    stage_s(pb)
                stage_bdq(b)
                if next_mod:
                    mod_weights(*mod, (2, 3))
                if k:
                    one_hot2(k)
                    if more:
                        one_hot(k + 1)
            if back:
                stage_W1(k - 1, "t", 1, (1,))
                product(pa, "h")
                stage_h(pa)
            else:
                steps(3)
            if front:
                stage_V(b)
                stage_O(a)
            if back:
                stage_uT(pb)
            if front:
                gather(a)
            if back:
                product(pb, "h")
                stage_h(pb)
            if front:
                stage_z(a)
                stage_v(a)
                if more:
                    stage_A(a + 2)
            if not back:
                steps(6)
            if front:
                stage_S(b)
                stage_S1(b)
                stage_max(b)
                stage_v2(a)
                if more:
                    stage_A1(a + 2)
            if back:
                stage_W1(k - 1, "s", 0)
            if not back:
                steps(4)
            if front:
                stage_E(b)
                stage_u(a)
                if more:
                    if not k:
                        load_x(b + 2)
                    stage_A2(a + 2)
                    split_x(b + 2)
            if not back:
                steps(4)
                stage_AV(b)
                stage_nT(b)
                steps(3)
                stage_aTr(b)
                stage_alo(b)
                stage_bdq(a + 2)
                steps(3)
                stage_V(a + 2)
                stage_O(b)
                steps(100)
                pro_end.extend([("Pm", 23), ("pbs", 0), ("s3_6", 3), ("wl", nw[0] - 1), ("wh", nw[0] - 1), ("wl", nw[0] - 2), *r_free["cr0"], *r_free["cr1"], ("dmp", 1)])
                slots[:] = slots[2:4]
                consts3()
                stage_zT(a)
                stage_uT(a)
                gather(b)
                product(a, "t")
                stage_t(a)
                table_P2()
                load_tok(2)
                load_tok(3)
                stage_x1T(a)
                stage_x1T2(a)
                stage_xbe(a)
                continue
            if back:
                stage_W1(k - 1, "s", 1)
            if front:
                stage_zT(a)
            if back:
                stage_W1(k - 1, "h", 0)
                stage_silu(k - 1, 0)
                stage_silu2(k - 1, 0)
                stage_W1(k - 1, "h", 1, (0,))
            if front:
                stage_AV(b)
            if back:
                stage_W1(k - 1, "h", 1, (1,))
                stage_silu(k - 1, 1)
                stage_silu2(k - 1, 1)
            if front:
                product(a, "t")
                stage_t(a)
                stage_nT(b)
                stage_uT(a)
                gather(b)
            if back:
                stage_W2a(pa)
                if not front:
                    stage_W2a(pb)
                stage_W2b(pa)
                if front:
                    stage_W2a(pb)
            if front:
                stage_aTr(b)
                stage_alo(b)
            if back:
                stage_out(pa)
            if more:
                stage_bdq(a + 2)
            if back:
                stage_W2b(pb)
                if not front:
                    stage_out(pb)
            if front:
                stage_O(b)
                stage_x1T(a)
                stage_x1T2(a)
                if more:
                    stage_V(a + 2)
                stage_xbe(a)
                if next_mod:
                    mod_load((a + 2) // 8, 1, (0, 1))
        for s in range(4):
            put("sp", None, None, [(f"out{s}", NG - 4 + s)])

        sems = {n: ctx.enter_context(nc.semaphore("s_" + n)) for n in Q.count}
        block = ctx.enter_context(nc.Block())

        @block.sync
        def _(e):
            Q.emit("sp", e, sems)

        @block.tensor
        def _(e):
            Q.emit("pe", e, sems)

        @block.scalar
        def _(e):
            Q.emit("act", e, sems)

        @block.vector
        def _(e):
            Q.emit("dve", e, sems)

        @block.gpsimd
        def _(e):
            Q.emit("pool", e, sems)


def kernel(**inp):
    import ml_dtypes
    import concourse.bacc as bacc
    from concourse.bass_utils import run_bass_kernel_spmd

    bf = ml_dtypes.bfloat16
    get = lambda n: np.asarray(inp[n])
    c = lambda x: np.ascontiguousarray(x)
    L0 = lambda n: get("L0_cond_" + n)
    L1 = lambda n: get("L1_cond_" + n)
    x = get("x").reshape(4096, 512)
    arr = {"x": c(x), "xT": c(x.reshape(NG, 128, 4, 128).transpose(0, 3, 2, 1))}

    def blocks(w, rows=None):
        n = w.shape[0]
        m = -(-n // 128)
        o = np.zeros((m * 128, w.shape[1]), w.dtype)
        o[:n] = w
        return c(o.reshape(m, 128, w.shape[1]))

    for s in "ko":
        arr[s + "_affT"] = blocks(L0(s + "_aff_w").T)
        arr[s + "_wT"] = blocks(L0(s + "_w").T)
    arr["affb"] = c(np.stack([L0("k_aff_b").reshape(4, 128).T, L0("o_aff_b").reshape(4, 128).T], 1))
    cond = np.zeros((4, 128, 4), np.float32)
    cond[0:2] = get("cond_512").T.reshape(2, 128, 4)
    cond[2, 0:64] = get("cond_64").T
    cond[3, 0:32] = get("fside_Bx32_0").T
    arr["condT"] = c(cond.transpose(1, 0, 2))

    def rows(*placed, times=3):
        o = np.zeros((128, 512), np.float32)
        for r, a in placed:
            a = a.reshape(-1, 512)
            for j in range(times):
                o[r + 8 * j:r + 8 * j + len(a)] = a
        return o

    arr["rows_b"] = rows((0, L0("k_b")), (32, L0("o_b")), (64, L1("int_b2")))
    arr["rows_t"], arr["rows_s"], arr["rows_h"] = rows((0, L1("tm_g"))), rows((32, L1("ms_g"))), rows((0, L1("cp_g")))
    arr["rows_p"] = rows((64, np.tile(L1("int_b1"), (4, 1))))
    arr["rows_v"] = np.stack([rows(*[(32 * i, np.tile(L1(n + t), (4, 1))) for i, n in enumerate(("mem", "noi", "res"))], times=1)
                              for t in ("_b1", "_b2", "_g", "_be")])
    tab = rows((0, L1("cp_b")), (32, L1("tm_b")), (64, L1("ms_b")), times=1)
    arr["tabT"] = c(tab.T.reshape(4, 128, 128).transpose(1, 0, 2))
    arr["pw"] = c(np.concatenate([L1("pw_g"), L1("pw_b")], 1))
    for n in ("int_g", "int_be", "aw"):
        arr[n] = c(L1(n))
    for n in ("mem", "noi", "res"):
        arr[n + "_w1"] = blocks(L1(n + "_W1"))
        arr[n + "_w2"] = blocks(L1(n + "_W2"))
    arr["int_w1"] = blocks(L1("int_W1"))
    arr["int_w2"] = blocks(L1("int_W2"))
    arr["cid"] = c(get("itok_BxS_0_4").reshape(-1))
    arr["sid"] = c(get("mask_BxS_ik0").reshape(-1))
    arr["pidx"] = c(get("itok_BxS_0_999").reshape(NG, 128).T)
    arr["bid"] = np.repeat(np.arange(4, dtype=np.int32), 1024)
    p = np.arange(128)
    cst = np.zeros((128, 5), np.float32)
    n_of = {0: 5, 1: 3, 2: 4, 3: 0}
    cst[:, 0] = [(i % 8) if (i % 32) < 24 and (i % 8) < n_of[i // 32] else -1 for i in p]
    for j in range(3):
        cst[:, 1 + j] = (p % 32) // 8 == j
    cst[:, 4] = -0.5
    arr["cst"] = cst
    arr["ident"] = np.eye(128, dtype=np.float32)
    arr["selT"] = c(np.broadcast_to((p[:, None] // 32 == np.arange(3)[None])[:, :, None], (128, 3, 128)).astype(bf))
    t2 = (p % 32) // 16
    arr["maskL"] = (np.where(p[:, None] == t2[None], np.float32(NEG), np.float32(0))).astype(bf)
    m = np.arange(32) // 16
    arr["maskR"] = ((p[:, None] != m[None]) & (p[:, None] < 2)).astype(bf)

    nc = bacc.Bacc("TRN2", target_bir_lowering=False, num_devices=1)
    A = {n: nc.dram_tensor("in_" + n, a.shape, mybir.dt.from_np(a.dtype), kind="ExternalInput").ap() for n, a in arr.items()}
    out = nc.dram_tensor("out", (4096, 512), F32, kind="ExternalOutput").ap()
    build(nc, A, out)
    r = run_bass_kernel_spmd(nc, [{"in_" + n: a for n, a in arr.items()}], core_ids=[0])
    return r.results[0]["out"].reshape(4, 1024, 512)
```
